# Optimizing a Trainium2 kernel written in Bass

```python
import numpy as np
import jax
import jax.numpy as jnp

def _softmax(x, axis=-1):
    return jax.nn.softmax(x, axis=axis)

def _gelu(x):
    return jax.nn.gelu(x, approximate=True)

def _silu(x):
    return jax.nn.silu(x)

def _sigmoid(x):
    return jax.nn.sigmoid(x)

def _layernorm(x, axis=-1, eps=1e-05):
    m = jnp.mean(x, axis=axis, keepdims=True)
    v = jnp.var(x, axis=axis, keepdims=True)
    return (x - m) / jnp.sqrt(v + eps)

def _scatter_add(tgt, idx, src, axis=0):
    return tgt.at[idx].add(src)

def _segment_sum(src, seg, n):
    return jax.ops.segment_sum(src, seg, n)
kernel_name = 'mk_conv_attn_hybrid_d2_conv_nchw384_r4_d7ed9b'

def setup_inputs(seed: int=0):
    np.random.seed(seed)
    _w = jnp.asarray

    def _rec_inputs():
        import jax
        import jax.numpy as jnp
        _gk = jax.random.key(seed)
        x = -0.0002221 + 1 * jax.random.normal(jax.random.fold_in(_gk, 1), (16, 96, 16, 16), jnp.float32)
        return x
    x = _rec_inputs()

    def _L0_conv_setup():
        import jax, jax.numpy as jnp
        import numpy as np
        from jax import lax
        FEAT = 48
        GROUP = 3
        B, H, W = (16, 16, 16)
        CIN = 2 * FEAT
        CGATE = 4 * FEAT

        def _group_ids(C, g=GROUP):
            return np.arange(C) * g // C

        def _mask_B(out_c, in_c, kw):
            og = _group_ids(out_c)[:, None]
            ig = _group_ids(in_c)[None, :]
            center = (og >= ig).astype(np.float32)
            m = np.zeros((out_c, in_c, 1, kw), dtype=np.float32)
            m[:, :, :, :kw // 2] = 1.0
            m[:, :, 0, kw // 2] = center
            return jnp.asarray(m)

        def _shuffle(h):
            b, c, hh, ww = h.shape
            return h.reshape(b, GROUP, 4, FEAT // GROUP, hh, ww).transpose(0, 2, 1, 3, 4, 5).reshape(b, c, hh, ww)
        key = jax.random.key(seed)
        k1, k2, k3, k4, k5 = jax.random.split(key, 5)
        x = jax.random.normal(k1, (B, CIN, H, W), dtype=jnp.float32)
        w_i2s = jax.random.normal(k2, (CGATE, CIN, 1, 3), dtype=jnp.float32) * 0.02
        w_s2s = jax.random.normal(k3, (CGATE, FEAT, 1, 3), dtype=jnp.float32) * 0.02
        w_skip = jax.random.normal(k4, (CIN, FEAT, 1, 1), dtype=jnp.float32) * 0.05
        b_skip = jax.random.normal(k5, (CIN,), dtype=jnp.float32) * 0.01
        return {'x': x, 'w_i2s': w_i2s, 'w_s2s': w_s2s, 'w_skip': w_skip, 'b_skip': b_skip}
    _L0_conv_all = _L0_conv_setup()
    _L0_conv_in = {k: v for k, v in _L0_conv_all.items() if k in ('w_i2s', 'w_s2s', 'w_skip', 'b_skip')}
    del _L0_conv_all

    def _L1_attn_setup():
        import jax, jax.numpy as jnp
        import numpy as np
        B, T, C = (16, 64, 96)
        H, HS = (6, 16)
        NEG_INF = jnp.finfo(jnp.float32).min
        key = jax.random.key(seed)
        ks = jax.random.split(key, 6)
        x = jax.random.normal(ks[0], (B, T, C), dtype=jnp.float32)
        Wq = jax.random.normal(ks[1], (H, C, HS), dtype=jnp.float32) * C ** (-0.5)
        Wk = jax.random.normal(ks[2], (H, C, HS), dtype=jnp.float32) * C ** (-0.5)
        Wv = jax.random.normal(ks[3], (H, C, HS), dtype=jnp.float32) * C ** (-0.5)
        Wp = jax.random.normal(ks[4], (H * HS, C), dtype=jnp.float32) * (H * HS) ** (-0.5)
        bp = jnp.zeros((C,), dtype=jnp.float32)
        return {'x': x, 'Wq': Wq, 'Wk': Wk, 'Wv': Wv, 'Wp': Wp, 'bp': bp}
    _L1_attn_all = _L1_attn_setup()
    _L1_attn_in = {k: v for k, v in _L1_attn_all.items() if k in ('Wq', 'Wk', 'Wv', 'Wp', 'bp')}
    del _L1_attn_all

    def _L1_ffn_setup():
        import jax, jax.numpy as jnp
        import numpy as np
        NUM_EXPERTS = 4
        TOP_K = 2
        DIM = 96
        HID = 4 * DIM
        key = jax.random.key(seed)
        ks = jax.random.split(key, 5)
        B, S = (16, 512)
        scale_in = 1.0 / np.sqrt(DIM)
        scale_hid = 1.0 / np.sqrt(HID)
        return {'x': jax.random.normal(ks[0], (B, S, DIM), dtype=jnp.float32), 'gate_w': jax.random.normal(ks[1], (DIM, NUM_EXPERTS), dtype=jnp.float32) * scale_in, 'gate_b': jnp.zeros((NUM_EXPERTS,), dtype=jnp.float32), 'w1': jax.random.normal(ks[2], (NUM_EXPERTS, DIM, HID), dtype=jnp.float32) * scale_in, 'b1': jnp.zeros((NUM_EXPERTS, HID), dtype=jnp.float32), 'w2': jax.random.normal(ks[3], (NUM_EXPERTS, HID, DIM), dtype=jnp.float32) * scale_hid, 'b2': jnp.zeros((NUM_EXPERTS, DIM), dtype=jnp.float32)}
    _L1_ffn_all = _L1_ffn_setup()
    _L1_ffn_in = {k: v for k, v in _L1_ffn_all.items() if k in ('gate_w', 'gate_b', 'w1', 'b1', 'w2', 'b2')}
    del _L1_ffn_all
    return {'x': x, 'L0_conv_w_i2s': _L0_conv_in['w_i2s'], 'L0_conv_w_s2s': _L0_conv_in['w_s2s'], 'L0_conv_w_skip': _L0_conv_in['w_skip'], 'L0_conv_b_skip': _L0_conv_in['b_skip'], 'L1_attn_Wq': _L1_attn_in['Wq'], 'L1_attn_Wk': _L1_attn_in['Wk'], 'L1_attn_Wv': _L1_attn_in['Wv'], 'L1_attn_Wp': _L1_attn_in['Wp'], 'L1_attn_bp': _L1_attn_in['bp'], 'L1_ffn_gate_w': _L1_ffn_in['gate_w'], 'L1_ffn_gate_b': _L1_ffn_in['gate_b'], 'L1_ffn_w1': _L1_ffn_in['w1'], 'L1_ffn_b1': _L1_ffn_in['b1'], 'L1_ffn_w2': _L1_ffn_in['w2'], 'L1_ffn_b2': _L1_ffn_in['b2']}

def reference(x, L0_conv_w_i2s, L0_conv_w_s2s, L0_conv_w_skip, L0_conv_b_skip, L1_attn_Wq, L1_attn_Wk, L1_attn_Wv, L1_attn_Wp, L1_attn_bp, L1_ffn_gate_w, L1_ffn_gate_b, L1_ffn_w1, L1_ffn_b1, L1_ffn_w2, L1_ffn_b2):
    import jax
    import jax.numpy as jnp

    def _L0_conv_ref(x, w_i2s, w_s2s, w_skip, b_skip):
        import jax, jax.numpy as jnp
        import numpy as np
        from jax import lax
        FEAT = 48
        GROUP = 3
        B, H, W = (16, 16, 16)
        CIN = 2 * FEAT
        CGATE = 4 * FEAT

        def _group_ids(C, g=GROUP):
            return np.arange(C) * g // C

        def _mask_B(out_c, in_c, kw):
            og = _group_ids(out_c)[:, None]
            ig = _group_ids(in_c)[None, :]
            center = (og >= ig).astype(np.float32)
            m = np.zeros((out_c, in_c, 1, kw), dtype=np.float32)
            m[:, :, :, :kw // 2] = 1.0
            m[:, :, 0, kw // 2] = center
            return jnp.asarray(m)

        def _shuffle(h):
            b, c, hh, ww = h.shape
            return h.reshape(b, GROUP, 4, FEAT // GROUP, hh, ww).transpose(0, 2, 1, 3, 4, 5).reshape(b, c, hh, ww)
        mask_i2s = _mask_B(CGATE, CIN, 3)
        mask_skip = _mask_B(CIN, FEAT, 1)
        h = lax.conv_general_dilated(x, w_i2s * mask_i2s, (1, 1), ((0, 0), (1, 1)), dimension_numbers=('NCHW', 'OIHW', 'NCHW'))
        h = _shuffle(h)
        w1 = w_s2s[:, :, 0, :]
        h_rows = h.transpose(2, 0, 1, 3)

        def step(carry, h_row):
            _h, c = carry
            s = lax.conv_general_dilated(_h, w1, (1,), ((1, 1),), dimension_numbers=('NCW', 'OIW', 'NCW')) + h_row
            o, f, i, g = jnp.split(jax.nn.sigmoid(s), 4, axis=1)
            c = f * c + i * g
            _h = o * jnp.tanh(c)
            return ((_h, c), _h)
        init = (jnp.zeros((B, FEAT, W), x.dtype), jnp.zeros((B, FEAT, W), x.dtype))
        _, out_h = lax.scan(step, init, h_rows)
        out_h = out_h.transpose(1, 2, 0, 3)
        skip = lax.conv_general_dilated(out_h, w_skip * mask_skip, (1, 1), ((0, 0), (0, 0)), dimension_numbers=('NCHW', 'OIHW', 'NCHW')) + b_skip[None, :, None, None]
        return x + skip

    def _L1_attn_ref(x, Wq, Wk, Wv, Wp, bp):
        import jax, jax.numpy as jnp
        import numpy as np
        B, T, C = (16, 64, 96)
        H, HS = (6, 16)
        NEG_INF = jnp.finfo(jnp.float32).min
        Bx, Tx, Cx = x.shape
        q = jnp.einsum('btc,hcd->bhtd', x, Wq)
        k = jnp.einsum('btc,hcd->bhtd', x, Wk)
        v = jnp.einsum('btc,hcd->bhtd', x, Wv)
        scores = jnp.einsum('bhtd,bhsd->bhts', q, k) * Cx ** (-0.5)
        causal = jnp.tril(jnp.ones((Tx, Tx), dtype=bool))
        scores = jnp.where(causal, scores, NEG_INF)
        weights = jax.nn.softmax(scores, axis=-1)
        out = jnp.einsum('bhts,bhsd->bhtd', weights, v)
        catted = out.transpose(0, 2, 1, 3).reshape(Bx, Tx, -1)
        return catted @ Wp + bp

    def _L1_ffn_ref(x, gate_w, gate_b, w1, b1, w2, b2):
        import jax, jax.numpy as jnp
        import numpy as np
        NUM_EXPERTS = 4
        TOP_K = 2
        DIM = 96
        HID = 4 * DIM
        scores = jnp.einsum('bsd,de->bse', x, gate_w) + gate_b
        probs = jax.nn.softmax(scores, axis=-1)
        topk_vals, topk_idx = jax.lax.top_k(probs, TOP_K)
        mask = jnp.sum(jax.nn.one_hot(topk_idx, NUM_EXPERTS, dtype=probs.dtype), axis=-2)
        masked = probs * mask
        masked = masked / (jnp.sum(masked, axis=-1, keepdims=True) + 1e-09)
        h = jax.nn.gelu(jnp.einsum('bsd,edh->ebsh', x, w1) + b1[:, None, None, :], approximate=False)
        y = jnp.einsum('ebsh,ehd->ebsd', h, w2) + b2[:, None, None, :]
        out = jnp.einsum('bse,ebsd->bsd', masked, y)
        return out

    def _gn(v, G=32, eps=1e-05):
        B_, C_, H_, W_ = v.shape
        g = v.reshape(B_, G, C_ // G, H_, W_)
        m = jnp.mean(g, axis=(2, 3, 4), keepdims=True)
        s = jnp.var(g, axis=(2, 3, 4), keepdims=True)
        return ((g - m) / jnp.sqrt(s + eps)).reshape(v.shape)

    def _ln_c(v, eps=1e-06):
        m = jnp.mean(v, axis=1, keepdims=True)
        s = jnp.var(v, axis=1, keepdims=True)
        return (v - m) / jnp.sqrt(s + eps)

    def _ln_t(v, eps=1e-05):
        m = jnp.mean(v, axis=-1, keepdims=True)
        s = jnp.var(v, axis=-1, keepdims=True)
        return (v - m) / jnp.sqrt(s + eps)

    def _to_tokens(v):
        B_, C_, H_, W_ = v.shape
        return v.reshape(B_, C_, H_ * W_).transpose(0, 2, 1)

    def _from_tokens(t, like):
        B_, C_, H_, W_ = like.shape
        return t.transpose(0, 2, 1).reshape(B_, C_, H_, W_)
    x = _L0_conv_ref(x, L0_conv_w_i2s, L0_conv_w_s2s, L0_conv_w_skip, L0_conv_b_skip)
    t = _to_tokens(x)
    t = t + _L1_attn_ref(_ln_t(t), L1_attn_Wq, L1_attn_Wk, L1_attn_Wv, L1_attn_Wp, L1_attn_bp)
    t = t + _L1_ffn_ref(_ln_t(t), L1_ffn_gate_w, L1_ffn_gate_b, L1_ffn_w1, L1_ffn_b1, L1_ffn_w2, L1_ffn_b2)
    x = _from_tokens(t, x)
    return x

_drawn_inputs = setup_inputs


def setup_inputs(seed=0):
    import zlib

    import numpy as np

    out = dict(_drawn_inputs(seed))
    spreads = {'L1_attn_bp': (0.0, 0.1),
     'L1_ffn_gate_b': (0.0, 0.1),
     'L1_ffn_b1': (0.0, 0.1),
     'L1_ffn_b2': (0.0, 0.1)}
    factors = {'L0_conv_w_s2s': 2.917}
    for name, (base, spread) in spreads.items():
        noise = np.random.default_rng([zlib.crc32(name.encode()), seed]).standard_normal(out[name].shape)
        drawn = base * np.exp(spread * noise) if base else spread * noise
        out[name] = jnp.asarray(drawn.astype(out[name].dtype))
    for name, factor in factors.items():
        out[name] = (out[name] * factor).astype(out[name].dtype)
    return out
```

```python
from contextlib import ExitStack

import concourse.bass as bass
from concourse import mybir

F32 = mybir.dt.float32
F32R = mybir.dt.float32r
BF16 = mybir.dt.bfloat16
ALU = mybir.AluOpType
ACT = mybir.ActivationFunctionType
AX = mybir.AxisListType

B, C, ROWS, W = 16, 96, 16, 16
FEAT = 48
PADW = W + 1
HPADW = W + 2
GATE_M = 64 + FEAT
HALF = B // 2
HC = HALF * W
HEADS, HS = 6, 16
VW = 32
TT = 128
SPB = 4
BT = SPB * TT
NBLK = B * ROWS * W // BT
HBLK = NBLK // 2
E, HID = 4, 384
NCH = E * HID // 128
CPE = HID // 128
SCALE = float(C) ** -0.5
GATE_STEPS = 14

HG = (3, 2)
UPS = (2, 3)
NU = (SPB * UPS[0], SPB * UPS[1])


def unit_base(n, half):
    return NU[0] * n if half == 0 else NU[1] * n - HBLK * (NU[1] - NU[0])


def hybrid_kernel(nc, x, wi, wi_mask, ws_a, ws_b, wk_skip, skip_mask, b_skip, wq, wk, wv, wp, bp,
                  gate_w, gate_b, w1, b1, w2, b2, ident, ident_bf, causal_bf, lower, out):
    with ExitStack() as ctx:
        def sb(name, shape, dt=F32):
            return ctx.enter_context(nc.sbuf_tensor(name, shape, dt))

        def bank(name):
            return ctx.enter_context(nc.psum_tensor(name, [128, 512], F32))

        def sem(name):
            return ctx.enter_context(nc.semaphore(name))

        id_sb = sb("id_sb", [128, 128])
        idb_sb = sb("idb_sb", [128, 128], BF16)
        causal_sb = sb("causal_sb", [128, HG[0], 128], BF16)
        lower_sb = sb("lower_sb", [128, E * E])
        wi_sb = sb("wi_sb", [C, 2, 2, GATE_M])
        wim_sb = sb("wim_sb", [C, 2, GATE_M])
        wsa_sb = sb("wsa_sb", [GATE_M, 2, GATE_M])
        wsb_sb = sb("wsb_sb", [FEAT, 2, GATE_M])
        wsk_sb = sb("wsk_sb", [FEAT, C])
        wskm_sb = sb("wskm_sb", [FEAT, C])
        bsk_sb = sb("bsk_sb", [C, 1])
        wraw = sb("wraw", [C, 2 * C + 128])
        whi = sb("whi", [C, 2 * C + 128], F32R)
        wlo = sb("wlo", [C, 2 * C + 128], F32R)
        wv_sb = sb("wv_sb", [C, C])
        wp_sb = sb("wp_sb", [C, 2, C])
        bp_sb = sb("bp_sb", [128, C])
        gb_sb = sb("gb_sb", [128, SPB * E])
        w1hi = sb("w1hi", [C, E * HID], F32R)
        w1lo = sb("w1lo", [C, E * HID], F32R)
        b1_sb = sb("b1_sb", [128, NCH])
        w2_sb = sb("w2_sb", [128, NCH, C])
        b2_sb = sb("b2_sb", [2, E * C])
        b2t = sb("b2t", [2, E * C], F32R)
        b2l = sb("b2l", [2, E * C])
        b2p = sb("b2p", [2, E * C])
        b2hl = sb("b2hl", [2, E * C], F32R)
        ones2 = sb("ones2", [2, 128], F32R)
        nhalf = sb("nhalf", [128, SPB])
        x_pad = sb("x_pad", [C, ROWS * B * PADW])
        h_pad = sb("h_pad", [GATE_M, B, HPADW])
        t_ig = sb("t_ig", [FEAT, 2, 2, HC])
        t_fg = sb("t_fg", [FEAT, 2, 2, HC])
        g1 = sb("g1", [FEAT, 2, HC])
        fc = sb("fc", [FEAT, 2, HC])
        ig = sb("ig", [FEAT, 2, HC])
        c4 = sb("c4", [FEAT, 2, HC])
        c2 = sb("c2", [FEAT, 2, HC])
        tc_sb = sb("tc_sb", [FEAT, 2, HC])
        t_cm = sb("t_cm", [C, NBLK * BT])
        t_st = sb("t_st", [C, BT])
        t0 = sb("t0", [128, SPB, C])
        tb = sb("tb", [128, SPB, C])
        st1 = sb("st1", [128, SPB, 6])
        mv1 = sb("mv1", [128, SPB, 2])
        ve1 = sb("ve1", [128, SPB])
        rs1 = sb("rs1", [128, SPB])
        xh = sb("xh", [128, SPB, C])
        x1hi = sb("x1hi", [C, BT], F32R)
        x1lo = sb("x1lo", [C, BT], F32R)
        x1f = sb("x1f", [C, BT])
        qhi = sb("qhi", [C, BT], F32R)
        qlo = sb("qlo", [C, BT], F32R)
        k_cur = sb("k_cur", [C, 2, BT], F32R)
        k_old = sb("k_old", [C, 2, HBLK * BT], F32R)
        k_bd = sb("k_bd", [C, 2, 2, HEADS, 2 * TT], F32R)
        v_cur = sb("v_cur", [128, SPB, HEADS, VW])
        v_old = sb("v_old", [128, HBLK, SPB * HEADS * VW])
        v_prev = sb("v_prev", [128, SPB, HEADS, VW])
        nmax = sb("nmax", [128, 2, HG[0]])
        den = sb("den", [128, 2, HG[0]])
        rden = sb("rden", [128, 2, HG[0]])
        p_sb = sb("p_sb", [128, 2, 512])
        pt_sb = sb("pt_sb", [128, 2, 512])
        o_t = sb("o_t", [C, 2, TT])
        t1 = sb("t1", [128, SPB, C])
        st2 = sb("st2", [128, SPB, 6])
        mv2 = sb("mv2", [128, SPB, 2])
        ve2 = sb("ve2", [128, SPB])
        rs2 = sb("rs2", [128, SPB])
        xh2 = sb("xh2", [128, SPB, C])
        x2hi = sb("x2hi", [C, BT], F32R)
        x2lo = sb("x2lo", [C, BT], F32R)
        gt_sb = sb("gt_sb", [E, BT])
        gl = sb("gl", [128, SPB, E])
        gm = sb("gm", [128, SPB])
        gd = sb("gd", [128, SPB, E])
        ge = sb("ge", [128, SPB, E])
        gtr = sb("gtr", [128, SPB, E, E])
        geq = sb("geq", [128, SPB, E, E])
        geo = sb("geo", [128, SPB, E, E])
        gbt = sb("gbt", [128, SPB, E, E])
        grk = sb("grk", [128, SPB, E])
        gkp = sb("gkp", [128, SPB, E])
        gs = sb("gs", [128, SPB])
        gs2 = sb("gs2", [128, SPB])
        gdn = sb("gdn", [128, SPB])
        grd = sb("grd", [128, SPB])
        gw = sb("gw", [128, SPB, E])
        hid = sb("hid", [128, NCH, BT])
        w1raw = hid[0:C, 0:3, :].rearrange("p a b -> p (a b)")
        y_sb = sb("y_sb", [128, SPB, C])

        G = bank("G")
        M = bank("M")
        A = bank("A")
        S = [bank("S0"), bank("S1")]
        T = bank("T")
        F = [bank("F0"), bank("F1")]

        gates_ready = sem("gates_ready")
        skip_ready = sem("skip_ready")
        tt_ready = sem("tt_ready")
        xt_ready = sem("xt_ready")
        q_ready = sem("q_ready")
        k_ready = sem("k_ready")
        v_ready = sem("v_ready")
        scores_ready = sem("scores_ready")
        pt_ready = sem("pt_ready")
        av_ready = sem("av_ready")
        proj_ready = sem("proj_ready")
        x2t_ready = sem("x2t_ready")
        route_ready = sem("route_ready")
        route_t_ready = sem("route_t_ready")
        hid_ready = sem("hid_ready")
        y_ready = sem("y_ready")
        gates_tanh = sem("gates_tanh")
        cell_tanh = sem("cell_tanh")
        t0_done = sem("t0_done")
        x1_copied = sem("x1_copied")
        qhi_done = sem("qhi_done")
        khi_done = sem("khi_done")
        v_done = sem("v_done")
        exp_done = sem("exp_done")
        ot_done = sem("ot_done")
        x2hi_done = sem("x2hi_done")
        route_copied = sem("route_copied")
        route_exp = sem("route_exp")
        gelu_done = sem("gelu_done")
        cell_dve = sem("cell_dve")
        h_ready = sem("h_ready")
        t_half = sem("t_half")
        ln1_stats = sem("ln1_stats")
        ln1_aggr = sem("ln1_aggr")
        xh_done = sem("xh_done")
        x1lo_done = sem("x1lo_done")
        qlo_done = sem("qlo_done")
        klo_done = sem("klo_done")
        max_done = sem("max_done")
        rden_done = sem("rden_done")
        pt_done = sem("pt_done")
        t1_done = sem("t1_done")
        ln2_stats = sem("ln2_stats")
        ln2_aggr = sem("ln2_aggr")
        xh2_done = sem("xh2_done")
        x2lo_done = sem("x2lo_done")
        route_dve = sem("route_dve")
        comb = sem("comb")
        scaled = sem("scaled")
        rs1_step = sem("rs1_step")
        rs2_step = sem("rs2_step")
        tb_done = sem("tb_done")
        w_rec_in = sem("w_rec_in")
        x_in = [sem(f"x_in{i}") for i in range(4)]
        w_in = sem("w_in")
        w1_in = sem("w1_in")
        t_staged = sem("t_staged")
        kbd_in = [sem("kbd_in0"), sem("kbd_in1")]
        k_kept = sem("k_kept")
        v_kept = sem("v_kept")
        v_back = sem("v_back")
        y_out = sem("y_out")
        zeroed = sem("zeroed")
        w_dve = sem("w_dve")
        w_act = sem("w_act")

        N_REC_W, N_W = 7, 17
        WSPLIT_ACT = 3
        block = ctx.enter_context(nc.Block())

        def x_row(r0, length=1):
            return x_pad[:, bass.ds(r0 * (B * PADW), B * PADW)].rearrange("p (b w) -> p b w", w=PADW)

        def kbd_total(n, half):
            a, b = 2 * HEADS * 16, 2 * 2 * HEADS * 16
            return a * (n + 1) if half == 0 else b * (n + 1) - HBLK * (b - a)

        def kbd_loaded(n, half, s):
            a, b = HEADS * 16, 2 * HEADS * 16
            per = (a, b)[half]
            before = 2 * a * n if half == 0 else 2 * b * n - 2 * HBLK * (b - a)
            return before + per * (s // 2 + 1)

        def wait_alone(eng, semaphore, value):
            if not isinstance(value, int):
                value = eng.snap(eng.to_reg(value))
            eng.wait_ge(zeroed, 5)
            eng.wait_ge(semaphore, value)

        def as_f32(ap):
            return ap.bitcast(F32)

        @block.sync
        def _(sp):
            for dst, src in ((wi_sb, wi), (wim_sb, wi_mask), (wsa_sb, ws_a), (wsb_sb, ws_b),
                             (wsk_sb, wk_skip), (wskm_sb, skip_mask), (bsk_sb, b_skip)):
                sp.dma_start(dst[:], src).then_inc(w_rec_in, 16)
            rows = ROWS * B * PADW // 4
            for i in range(4):
                sp.dma_start(x_pad[:, i * rows:(i + 1) * rows], x[:, i * rows:(i + 1) * rows]).then_inc(x_in[i], 16)
                if i == 0:
                    for dst, src in ((id_sb[:], ident), (idb_sb[:], ident_bf), (causal_sb[:], causal_bf),
                                     (lower_sb[:], lower), (wraw[:, 0:C], wq), (wraw[:, C:2 * C], wk),
                                     (wraw[:, 2 * C:], gate_w), (wv_sb[:], wv), (wp_sb[:], wp), (bp_sb[:], bp),
                                     (gb_sb[:], gate_b), (b1_sb[:], b1), (b2_sb[:], b2), (w2_sb[:], w2)):
                        sp.dma_start(dst, src).then_inc(w_in, 16)
                    sp.dma_start(w1raw, w1).then_inc(w1_in, 16)

            def stage(n):
                sp.dma_start(t_st[:], t_cm[:, bass.ds(n * BT, BT)]).then_inc(t_staged, 16)

            def load_keys(n, half, s):
                for h in range(HEADS):
                    rows_h = slice(h * HS, (h + 1) * HS)
                    if half:
                        src = k_old[rows_h, :, bass.ds((n - HBLK) * BT + s * TT, TT)]
                        sp.dma_start(as_f32(k_bd[rows_h, s % 2, :, h, 0:TT]), as_f32(src)).then_inc(kbd_in[s % 2], 16)
                    sp.dma_start(as_f32(k_bd[rows_h, s % 2, :, h, half * TT:(half + 1) * TT]),
                                 as_f32(k_cur[rows_h, :, s * TT:(s + 1) * TT])).then_inc(kbd_in[s % 2], 16)

            def store_y(n):
                wait_alone(sp, comb, 16 * n + 16)
                sp.dma_start(out[bass.ds(n, 1)].rearrange("a p s c -> p (a s) c"), y_sb[:]).then_inc(y_out, 16)

            def body(n, half, first=False, last=False):
                ub = unit_base(n, half)
                wait_alone(sp, klo_done, n + 1)
                if not first:
                    wait_alone(sp, scores_ready, ub)
                load_keys(n, half, 0)
                load_keys(n, half, 1)
                if half == 0:
                    sp.dma_start(as_f32(k_old[:, :, bass.ds(n * BT, BT)]), as_f32(k_cur[:])).then_inc(k_kept, 16)
                    wait_alone(sp, v_done, n + 1)
                    sp.dma_start(v_old[:, bass.ds(n, 1), :], v_cur[:].rearrange("p (o s) h w -> p o (s h w)", o=1)
                                 ).then_inc(v_kept, 16)
                for s in (2, 3):
                    wait_alone(sp, scores_ready, ub + (s - 1) * UPS[half])
                    load_keys(n, half, s)
                if not first:
                    store_y(n - 1)
                if not last:
                    stage_next(n, half)

            def stage_next(n, half):
                sp.wait_ge(tt_ready, n + 1)
                if half == 0:
                    wait_alone(sp, t_half, 16 + 4 * n + 4)
                stage(n + 1)

            sp.wait_ge(zeroed, 5)
            sp.wait_ge(t_half, 16)
            stage(0)
            body(0, 0, first=True)
            with sp.Fori(1, HBLK) as n:
                body(n, 0)
            sp.wait_ge(k_kept, 16 * HBLK)
            sp.wait_ge(v_kept, 16 * HBLK)

            def fetch_values(n):
                sp.dma_start(v_prev[:].rearrange("p (o s) h w -> p o (s h w)", o=1),
                             v_old[:, bass.ds(n - HBLK, 1), :]).then_inc(v_back, 16)

            with sp.Fori(HBLK, NBLK - 1) as n:
                fetch_values(n)
                body(n, 1)
                wait_alone(sp, av_ready, unit_base(n, 1) + NU[1])
            fetch_values(NBLK - 1)
            body(NBLK - 1, 1, last=True)
            store_y(NBLK - 1)
            sp.wait_ge(y_out, 16 * NBLK)

        @block.gpsimd
        def _(pool):
            nc.gpsimd.memset(h_pad[:], 0.0).then_inc(zeroed, 1)
            nc.gpsimd.memset(c2[:], 0.0).then_inc(zeroed, 1)
            nc.gpsimd.memset(as_f32(k_bd[:]), 0.0).then_inc(zeroed, 1)
            nc.gpsimd.memset(v_cur[:], 0.0).then_inc(zeroed, 1)
            nc.gpsimd.memset(nhalf[:], -0.5).then_inc(zeroed, 1)
            pool.wait_ge(zeroed, 5)

            def rstd1(n):
                wait_alone(pool, ln1_aggr, 4 * n + 4)
                nc.gpsimd.tensor_scalar(ve1[:], mv1[:, :, 1], 1e-5, None, ALU.add).then_inc(rs1_step, 1)
                pool.wait_ge(rs1_step, 2 * n + 1)
                nc.gpsimd.tensor_tensor(rs1[:], ve1[:], nhalf[:], ALU.pow).then_inc(rs1_step, 1)

            def rstd2(n, s):
                wait_alone(pool, ln2_aggr, 4 * n + s + 1)
                nc.gpsimd.tensor_scalar(ve2[:, s:s + 1], mv2[:, s, 1:2], 1e-5, None, ALU.add).then_inc(rs2_step, 1)
                pool.wait_ge(rs2_step, 8 * n + 2 * s + 1)
                nc.gpsimd.tensor_tensor(rs2[:, s:s + 1], ve2[:, s:s + 1], nhalf[:, 0:1], ALU.pow).then_inc(rs2_step, 1)

            def residual(n):
                pool.wait_ge(t0_done, n + 1)
                nc.gpsimd.tensor_tensor(tb[:], t0[:], bp_sb[:].unsqueeze(1).to_broadcast((128, SPB, C)),
                                        ALU.add).then_inc(tb_done, 1)

            def scale(n, half, u):
                wait_alone(pool, rden_done, unit_base(n, half) + u + 1)
                nk = TT * (half + 1)
                for i in range(HG[half]):
                    p = p_sb[:, u % 2, i * nk:(i + 1) * nk]
                    last = nc.gpsimd.tensor_scalar(p, p, rden[:, u % 2, i:i + 1], 1.0, ALU.mult, ALU.mult)
                last.then_inc(scaled, 1)

            def body(n, half, last=False):
                for u in range(NU[half]):
                    scale(n, half, u)
                    for s in range(SPB - 1):
                        if u == (s + 1) * UPS[half] + 2 and u < NU[half] or (u == NU[half] - 1 and (s + 1) * UPS[half] + 2 > u):
                            rstd2(n, s)
                if not last:
                    rstd1(n + 1)
                rstd2(n, SPB - 1)
                if not last:
                    pool.wait_ge(t1_done, 4 * n + 4)
                    residual(n + 1)

            pool.wait_ge(w_in, 16 * 14)
            rstd1(0)
            residual(0)
            with pool.Fori(0, HBLK) as n:
                body(n, 0)
            with pool.Fori(HBLK, NBLK - 1) as n:
                body(n, 1)
            body(NBLK - 1, 1, last=True)

        @block.scalar
        def _(act):
            def cell_gates(m, hb, src):
                act.wait_ge(gates_ready, m + 1)
                v = src[:, 0:2 * HC].rearrange("p (c n) -> p c n", c=2)
                nc.scalar.activation(t_fg[:, hb], v[64:64 + FEAT], ACT.Tanh, scale=0.5).then_inc(gates_tanh, 1)
                nc.scalar.activation(t_ig[:, hb], v[0:FEAT], ACT.Tanh, scale=0.5).then_inc(gates_tanh, 1)

            def cell_out(m, hb):
                act.wait_ge(cell_dve, 5 * m + 4)
                nc.scalar.activation(tc_sb[:, hb], c4[:, hb], ACT.Tanh, scale=0.25).then_inc(cell_tanh, 1)

            def rec0(it):
                for q in range(4):
                    m = 4 * it + q
                    cell_gates(m, q % 2, (G, A)[q % 2])
                    cell_out(m, q % 2)

            act.wait_ge(w_in, 16 * 14)
            nc.scalar.copy(whi[:], wraw[:]).then_inc(w_act, 1)
            nc.scalar.copy(b2t[:], b2_sb[:]).then_inc(w_act, 1)
            act.wait_ge(w1_in, 16)
            nc.scalar.copy(w1hi[:], w1raw).then_inc(w_act, 1)
            with act.Fori(0, 4) as it:
                rec0(it)

            def project_t0(n):
                act.wait_ge(tt_ready, n + 1)
                nc.scalar.copy(t0[:], S[0][:, 0:SPB * C].rearrange("p (s c) -> p s c", s=SPB)).then_inc(t0_done, 1)

            def project_rest(n):
                act.wait_ge(xt_ready, n + 1)
                nc.scalar.copy(x1hi[:], S[1][0:C, :]).then_inc(x1_copied, 1)
                nc.scalar.copy(x1f[:], S[1][0:C, :]).then_inc(x1_copied, 1)

            def project_qkv(n):
                act.wait_ge(q_ready, n + 1)
                nc.scalar.mul(qhi[:], S[0][0:C, :], SCALE).then_inc(qhi_done, 1)
                act.wait_ge(k_ready, n + 1)
                nc.scalar.copy(k_cur[:, 0, :], S[1][0:C, :]).then_inc(khi_done, 1)
                act.wait_ge(v_ready, n + 1)
                nc.scalar.copy(v_cur[:, :, :, 0:HS],
                               S[0][:, 0:SPB * C].rearrange("p (s h d) -> p s h d", s=SPB, h=HEADS)).then_inc(v_done, 1)

            def exps(n, half, u):
                ub = unit_base(n, half)
                act.wait_ge(max_done, ub + u + 1)
                if u >= 2 or not isinstance(n, int) or n > 0:
                    act.wait_ge(pt_ready, ub + u - 1)
                nk = TT * (half + 1)
                for i in range(HG[half]):
                    last = nc.scalar.activation(p_sb[:, u % 2, i * nk:(i + 1) * nk], S[u % 2][:, i * nk:(i + 1) * nk],
                                                ACT.Exp, bias=nmax[:, u % 2, i:i + 1],
                                                accum_out=den[:, u % 2, i:i + 1])
                last.then_inc(exp_done, 1)

            def heads_out(n, half, s):
                act.wait_ge(av_ready, unit_base(n, half) + (s + 1) * UPS[half])
                if s or not isinstance(n, int) or n > 0:
                    act.wait_ge(proj_ready, 4 * n + s)
                nc.scalar.copy(o_t[:], A[0:C, 0:2 * TT].rearrange("p (a t) -> p a t", a=2)).then_inc(ot_done, 1)

            def body(n, half, first=False, last=False):
                if not first:
                    act.wait_ge(route_dve, GATE_STEPS * (n - 1) + 3)
                    nc.scalar.activation(ge[:], gd[:], ACT.Exp).then_inc(route_exp, 1)
                exps(n, half, 0)
                for j in range(NU[half]):
                    if j + 1 < NU[half]:
                        exps(n, half, j + 1)
                    if j % UPS[half] == 0 and j:
                        heads_out(n, half, j // UPS[half] - 1)
                    if half == 0:
                        m = 16 + 4 * n + j // 2
                        if j % 2 == 0:
                            cell_gates(m, (j // 2) % 2, G)
                        else:
                            cell_out(m, (j // 2) % 2)
                heads_out(n, half, SPB - 1)
                if not last:
                    project_t0(n + 1)
                    project_rest(n + 1)
                act.wait_ge(x2t_ready, n + 1)
                nc.scalar.copy(x2hi[:], T[0:C, :]).then_inc(x2hi_done, 1)
                if not last:
                    act.wait_ge(kbd_in[0], kbd_total(n, half))
                    act.wait_ge(kbd_in[1], kbd_total(n, half))
                    if half == 0:
                        act.wait_ge(k_kept, 16 * n + 16)
                        act.wait_ge(v_kept, 16 * n + 16)
                    project_qkv(n + 1)
                act.wait_ge(route_ready, n + 1)
                nc.scalar.copy(gt_sb[:], M[0:E, :]).then_inc(route_copied, 1)
                if not first:
                    act.wait_ge(y_ready, 4 * n)
                for c in range(NCH):
                    act.wait_ge(hid_ready, NCH * n + c + 1)
                    nc.scalar.activation(hid[:, c, :], F[c % 2][:], ACT.Gelu, bias=b1_sb[:, c:c + 1]
                                         ).then_inc(gelu_done, 1)

            project_t0(0)
            project_rest(0)
            project_qkv(0)
            body(0, 0, first=True)
            with act.Fori(1, HBLK) as n:
                body(n, 0)
            with act.Fori(HBLK, NBLK - 1) as n:
                body(n, 1)
            body(NBLK - 1, 1, last=True)
            act.wait_ge(route_dve, GATE_STEPS * (NBLK - 1) + 3)
            nc.scalar.activation(ge[:], gd[:], ACT.Exp).then_inc(route_exp, 1)

        @block.vector
        def _(dve):
            V = nc.vector
            steps = [0]

            def setup_step(ins):
                steps[0] += 1
                ins.then_inc(w_dve, 1)

            dve.wait_ge(w_rec_in, 16 * N_REC_W)
            setup_step(V.tensor_tensor(wi_sb[:, 1], wi_sb[:, 1], wim_sb[:], ALU.mult))
            setup_step(V.tensor_scalar(wsa_sb[:], wsa_sb[:], 0.5, None, ALU.mult))
            setup_step(V.tensor_scalar(wsb_sb[:], wsb_sb[:], 0.5, None, ALU.mult))
            setup_step(V.scalar_tensor_tensor(wsk_sb[:], wsk_sb[:], 0.5, wskm_sb[:], ALU.mult, ALU.mult))
            setup_step(V.memset(as_f32(ones2[:]), 1.0))
            dve.wait_ge(w_act, WSPLIT_ACT)
            setup_step(V.tensor_tensor(wlo[:], wraw[:], as_f32(whi[:]), ALU.subtract))
            setup_step(V.tensor_tensor(w1lo[:], w1raw, as_f32(w1hi[:]), ALU.subtract))
            setup_step(V.tensor_tensor(b2l[:], b2_sb[:], as_f32(b2t[:]), ALU.subtract))
            setup_step(V.tensor_scalar(b2p[:], as_f32(b2t[:]), id_sb[0:2, 0:1], None, ALU.mult))
            dve.wait_ge(w_dve, 9)
            setup_step(V.scalar_tensor_tensor(b2hl[:], b2l[:], id_sb[0:2, 1:2], b2p[:], ALU.mult, ALU.add))
            dve.wait_ge(zeroed, 5)

            def cell(m, hb):
                dve.wait_ge(gates_tanh, 2 * m + 1)
                V.tensor_scalar(g1[:, hb], t_fg[:, hb, 1], 1.0, None, ALU.add).then_inc(cell_dve, 1)
                V.scalar_tensor_tensor(fc[:, hb], t_fg[:, hb, 0], 1.0, c2[:, hb], ALU.add, ALU.mult).then_inc(cell_dve, 1)
                dve.wait_ge(gates_tanh, 2 * m + 2)
                dve.wait_ge(cell_dve, 5 * m + 1)
                V.scalar_tensor_tensor(ig[:, hb], t_ig[:, hb, 1], 1.0, g1[:, hb], ALU.add, ALU.mult).then_inc(cell_dve, 1)
                dve.wait_ge(cell_dve, 5 * m + 3)
                V.tensor_tensor(c4[:, hb], fc[:, hb], ig[:, hb], ALU.add).then_inc(cell_dve, 1)
                dve.wait_ge(cell_dve, 5 * m + 4)
                V.tensor_scalar(c2[:, hb], c4[:, hb], 0.5, None, ALU.mult).then_inc(cell_dve, 1)

            def cell_h(m, hb, first=False):
                dve.wait_ge(cell_tanh, m + 1)
                if not first:
                    dve.wait_ge(skip_ready, m - 1)
                o = t_ig[:, hb, 0].rearrange("p (b w) -> p b w", w=W)
                t = tc_sb[:, hb].rearrange("p (b w) -> p b w", w=W)
                bs = slice(hb * HALF, (hb + 1) * HALF)
                V.scalar_tensor_tensor(h_pad[0:FEAT, bs, 1:1 + W], o, 1.0, t, ALU.add, ALU.mult).then_inc(h_ready, 1)
                V.scalar_tensor_tensor(h_pad[64:64 + FEAT, bs, 0:W], o, 1.0, t, ALU.add, ALU.mult).then_inc(h_ready, 1)

            def add_skip(m, hb, row, half, row8):
                dve.wait_ge(skip_ready, m + 1)
                dst = t_cm[:, bass.ds(row8 * W + half * HBLK * BT, (B - 1) * TT + W)]
                dst = t_rows(half, row8)[:, hb * HALF:(hb + 1) * HALF, :]
                xr = x_row(row)[:, hb * HALF:(hb + 1) * HALF, 1:]
                V.scalar_tensor_tensor(dst, M[0:C, hb * HC:(hb + 1) * HC].rearrange("p (b w) -> p b w", w=W),
                                       bsk_sb[:, 0:1], xr, ALU.add, ALU.add).then_inc(t_half, 1)

            def t_rows(half, row8):
                v = t_cm[:, half * HBLK * BT:(half + 1) * HBLK * BT].rearrange("p (b t) -> p b t", t=TT)
                return v[:, :, bass.ds(row8 * W, W)]

            def rec0(it, first):
                for q in range(4):
                    m, hb = 4 * it + q, q % 2
                    cell(m, hb)
                    if q >= 2 or not first:
                        row = 2 * it + q // 2 - 1
                        add_skip(m - 2, hb, row, 0, row)
                    cell_h(m, hb, first=first and q < 2)

            dve.wait_ge(x_in[0], 16)
            rec0(0, True)
            for i in (1, 2, 3):
                dve.wait_ge(x_in[i], 16)
            with dve.Fori(1, 4) as it:
                rec0(it, False)
            for hb in range(2):
                add_skip(14 + hb, hb, 7, 0, 7)

            def norm1(n):
                dve.wait_ge(t0_done, n + 1)
                for s in range(SPB):
                    V.bn_stats(st1[:, s], t0[:, s]).then_inc(ln1_stats, 1)
                wait_alone(dve, ln1_stats, 4 * n + 4)
                for s in range(SPB):
                    V.bn_aggr(mv1[:, s], st1[:, s]).then_inc(ln1_aggr, 1)

            def normalize1(n):
                dve.wait_ge(rs1_step, 2 * n + 2)
                for s in range(SPB):
                    V.tensor_scalar(xh[:, s], t0[:, s], mv1[:, s, 0:1], rs1[:, s:s + 1],
                                    ALU.subtract, ALU.mult).then_inc(xh_done, 1)

            def x1_rest(n):
                dve.wait_ge(x1_copied, 2 * n + 2)
                V.tensor_tensor(x1lo[:], S[1][0:C, :], as_f32(x1hi[:]), ALU.subtract).then_inc(x1lo_done, 1)

            def qk_rest(n):
                dve.wait_ge(qhi_done, n + 1)
                V.scalar_tensor_tensor(qlo[:], S[0][0:C, :], SCALE, as_f32(qhi[:]), ALU.mult, ALU.subtract
                                       ).then_inc(qlo_done, 1)
                dve.wait_ge(khi_done, n + 1)
                V.tensor_tensor(k_cur[:, 1, :], S[1][0:C, :], as_f32(k_cur[:, 0, :]), ALU.subtract
                                ).then_inc(klo_done, 1)

            def row_max(n, half, u):
                ub = unit_base(n, half)
                nk = TT * (half + 1)
                dve.wait_ge(scores_ready, ub + u + 1)
                V.tensor_reduce(nmax[:, u % 2, 0:HG[half]],
                                S[u % 2][:, 0:HG[half] * nk].rearrange("p (h k) -> p h k", k=nk),
                                AX.X, ALU.max, negate=True).then_inc(max_done, 1)

            def recip(n, half, u):
                dve.wait_ge(exp_done, unit_base(n, half) + u + 1)
                V.reciprocal(rden[:, u % 2, 0:HG[half]], den[:, u % 2, 0:HG[half]]).then_inc(rden_done, 1)

            def take_pt(n, half, u):
                ub = unit_base(n, half)
                w = HG[half] * (half + 1) * TT
                dve.wait_ge(pt_ready, ub + u + 1)
                if u >= 2 or not isinstance(n, int) or n > 0:
                    dve.wait_ge(av_ready, ub + u - 1)
                V.tensor_copy(pt_sb[:, u % 2, 0:w], T[:, 0:w]).then_inc(pt_done, 1)

            def attn_residual(n, s):
                dve.wait_ge(proj_ready, 4 * n + s + 1)
                dve.wait_ge(tb_done, n + 1)
                V.tensor_tensor(t1[:, s], M[:, 0:C], tb[:, s], ALU.add).then_inc(t1_done, 1)
                dve.wait_ge(t1_done, 4 * n + s + 1)
                V.bn_stats(st2[:, s], t1[:, s]).then_inc(ln2_stats, 1)
                wait_alone(dve, ln2_stats, 4 * n + s + 1)
                V.bn_aggr(mv2[:, s], st2[:, s]).then_inc(ln2_aggr, 1)

            def normalize2(n, s):
                dve.wait_ge(rs2_step, 8 * n + 2 * s + 2)
                V.tensor_scalar(xh2[:, s], t1[:, s], mv2[:, s, 0:1], rs2[:, s:s + 1],
                                ALU.subtract, ALU.mult).then_inc(xh2_done, 1)

            def route(n, part):
                base = GATE_STEPS * n
                ej = (128, SPB, E, E)
                of_j = ge[:].unsqueeze(2).to_broadcast(ej)
                of_e = ge[:].unsqueeze(3).to_broadcast(ej)
                if part == 0:
                    dve.wait_ge(route_t_ready, n + 1)
                    V.tensor_tensor(gl[:].rearrange("p s e -> p (s e)"), M[:, 0:SPB * E], gb_sb[:], ALU.add
                                    ).then_inc(route_dve, 1)
                    dve.wait_ge(route_dve, base + 1)
                    V.tensor_reduce(gm[:], gl[:], AX.X, ALU.max).then_inc(route_dve, 1)
                    dve.wait_ge(route_dve, base + 2)
                    V.tensor_tensor(gd[:], gl[:], gm[:].unsqueeze(2).to_broadcast((128, SPB, E)), ALU.subtract
                                    ).then_inc(route_dve, 1)
                    return
                dve.wait_ge(route_exp, n + 1)
                V.tensor_tensor(gtr[:], of_j, of_e, ALU.is_gt).then_inc(route_dve, 1)
                V.tensor_tensor(geq[:], of_j, of_e, ALU.is_equal).then_inc(route_dve, 1)
                dve.wait_ge(route_dve, base + 5)
                V.tensor_tensor(geo[:].rearrange("p s e j -> p s (e j)"), geq[:].rearrange("p s e j -> p s (e j)"),
                                lower_sb[:].unsqueeze(1).to_broadcast((128, SPB, E * E)), ALU.mult).then_inc(route_dve, 1)
                dve.wait_ge(route_dve, base + 6)
                V.tensor_tensor(gbt[:], gtr[:], geo[:], ALU.add).then_inc(route_dve, 1)
                dve.wait_ge(route_dve, base + 7)
                V.tensor_reduce(grk[:], gbt[:], AX.X, ALU.add).then_inc(route_dve, 1)
                dve.wait_ge(route_dve, base + 8)
                V.scalar_tensor_tensor(gkp[:], grk[:], 1.5, ge[:], ALU.is_lt, ALU.mult).then_inc(route_dve, 1)
                V.tensor_reduce(gs[:], ge[:], AX.X, ALU.add).then_inc(route_dve, 1)
                dve.wait_ge(route_dve, base + 10)
                V.tensor_reduce(gs2[:], gkp[:], AX.X, ALU.add).then_inc(route_dve, 1)
                dve.wait_ge(route_dve, base + 11)
                V.scalar_tensor_tensor(gdn[:], gs[:], 1e-9, gs2[:], ALU.mult, ALU.add).then_inc(route_dve, 1)
                dve.wait_ge(route_dve, base + 12)
                V.reciprocal(grd[:], gdn[:]).then_inc(route_dve, 1)
                dve.wait_ge(route_dve, base + 13)
                V.tensor_tensor(gw[:], gkp[:], grd[:].unsqueeze(2).to_broadcast((128, SPB, E)), ALU.mult
                                ).then_inc(route_dve, 1)
                dve.wait_ge(route_dve, base + 14)

            def combine(n, s, first=False):
                dve.wait_ge(y_ready, 4 * n + s + 1)
                if s == 0 and not first:
                    dve.wait_ge(y_out, 16 * n)
                for e in range(E):
                    if e:
                        dve.wait_ge(comb, 16 * n + 4 * s + e)
                    V.scalar_tensor_tensor(y_sb[:, s], F[s % 2][:, e * C:(e + 1) * C], gw[:, s, e:e + 1],
                                           t1[:, s] if e == 0 else y_sb[:, s], ALU.mult, ALU.add).then_inc(comb, 1)

            def body(n, half, first=False, second=False, last=False):
                ups, nu = UPS[half], NU[half]
                row_max(n, half, 0)
                row_max(n, half, 1)
                recip(n, half, 0)
                if not first:
                    route(n - 1, 1)
                for j in range(nu):
                    if j + 1 < nu:
                        recip(n, half, j + 1)
                    take_pt(n, half, j)
                    if j + 2 < nu:
                        row_max(n, half, j + 2)
                    for s in range(SPB):
                        if not first and j == (s + 1) * ups:
                            combine(n - 1, s, first=second)
                        if j == (s + 1) * ups + 1:
                            attn_residual(n, s)
                        if j == (s + 1) * ups + 2:
                            normalize2(n, s)
                    if half == 0:
                        q = j // 2
                        m = 16 + 4 * n + q
                        if j % 2 == 0:
                            if q:
                                add_skip(m - 1, (q - 1) % 2, 8 + 2 * n + (q - 1) // 2, 1, 2 * n + (q - 1) // 2)
                            cell(m, q % 2)
                        else:
                            cell_h(m, q % 2)
                if not first:
                    combine(n - 1, SPB - 1)
                if half == 0:
                    add_skip(16 + 4 * n + 3, 1, 8 + 2 * n + 1, 1, 2 * n + 1)
                for s in range(SPB - 1):
                    if (s + 1) * ups + 2 >= nu:
                        normalize2(n, s)
                if not last:
                    norm1(n + 1)
                attn_residual(n, SPB - 1)
                if not last:
                    normalize1(n + 1)
                normalize2(n, SPB - 1)
                if not last:
                    x1_rest(n + 1)
                dve.wait_ge(x2hi_done, n + 1)
                V.tensor_tensor(x2lo[:], T[0:C, :], as_f32(x2hi[:]), ALU.subtract).then_inc(x2lo_done, 1)
                if not last:
                    qk_rest(n + 1)
                route(n, 0)

            norm1(0)
            normalize1(0)
            x1_rest(0)
            qk_rest(0)
            body(0, 0, first=True)
            body(1, 0, second=True)
            with dve.Fori(2, HBLK) as n:
                body(n, 0)
            with dve.Fori(HBLK, NBLK - 1) as n:
                body(n, 1)
            body(NBLK - 1, 1, last=True)
            route(NBLK - 1, 1)
            for s in range(SPB):
                combine(NBLK - 1, s)

        @block.tensor
        def _(pe):
            mm = nc.tensor.matmul

            def split3(dst, hi_l, lo_l, hi_r, lo_r, stop=True, **kw):
                mm(dst, hi_l, hi_r, start=True, stop=False, **kw)
                mm(dst, hi_l, lo_r, start=False, stop=False, **kw)
                return mm(dst, lo_l, hi_r, start=False, stop=stop, **kw)

            def gates(m, hb, row, dst, free, first=False):
                bs = slice(hb * HALF, (hb + 1) * HALF)
                if free is not None:
                    pe.wait_ge(gates_tanh, free)
                xr = x_row(row)
                for c in range(2):
                    for tap in range(2):
                        last = mm(dst[0:GATE_M, c * HC:(c + 1) * HC], wi_sb[:, tap, c], xr[:, bs, tap:tap + W],
                                  start=(c == 0 and tap == 0), stop=False, skip_group_check=True)
                if not first:
                    pe.wait_ge(h_ready, 2 * m - 2)
                for c in range(2):
                    d = dst[0:GATE_M, c * HC:(c + 1) * HC]
                    mm(d, wsa_sb[:, c], h_pad[:, bs, 0:W], start=False, stop=False, skip_group_check=True)
                    last = mm(d, wsb_sb[:, c], h_pad[0:FEAT, bs, 2:2 + W], start=False, stop=True, skip_group_check=True)
                last.then_inc(gates_ready, 1)

            def skip(m, hb):
                pe.wait_ge(h_ready, 2 * m + 2)
                bs = slice(hb * HALF, (hb + 1) * HALF)
                mm(M[0:C, hb * HC:(hb + 1) * HC], wsk_sb[:], h_pad[0:FEAT, bs, 1:1 + W], start=True, stop=True
                   ).then_inc(skip_ready, 1)

            def rec0(it, first):
                for q in range(4):
                    m, hb = 4 * it + q, q % 2
                    started = q >= 2 or not first
                    gates(m, hb, 2 * it + q // 2, (G, A)[hb], 2 * m - 2 if started else None, first=not started)
                    if started:
                        if q >= 3 or not first:
                            pe.wait_ge(t_half, m - 2)
                        skip(m - 2, hb)

            pe.wait_ge(w_dve, 4)
            pe.wait_ge(zeroed, 5)
            pe.wait_ge(x_in[0], 16)
            rec0(0, True)
            for i in (1, 2, 3):
                pe.wait_ge(x_in[i], 16)
            with pe.Fori(1, 4) as it:
                rec0(it, False)
            for hb in range(2):
                pe.wait_ge(t_half, 14 + hb)
                skip(14 + hb, hb)
            pe.wait_ge(w_dve, 10)
            pe.wait_ge(w_in, 16 * 14)

            def tokens_first(n):
                pe.wait_ge(t_staged, 16 * n + 16)
                for s in range(SPB):
                    last = nc.tensor.transpose(S[0][:, s * C:(s + 1) * C], t_st[:, s * TT:(s + 1) * TT], id_sb[0:C, 0:C])
                last.then_inc(tt_ready, 1)

            def channels_first(n):
                pe.wait_ge(xh_done, 4 * n + 4)
                for s in range(SPB):
                    last = nc.tensor.transpose(S[1][0:C, s * TT:(s + 1) * TT], xh[:, s], id_sb[:])
                last.then_inc(xt_ready, 1)

            def project(n):
                pe.wait_ge(x1lo_done, n + 1)
                pe.wait_ge(t0_done, n + 1)
                split3(S[0][0:C, :], whi[:, 0:C], wlo[:, 0:C], x1hi[:], x1lo[:]).then_inc(q_ready, 1)
                split3(S[1][0:C, :], whi[:, C:2 * C], wlo[:, C:2 * C], x1hi[:], x1lo[:]).then_inc(k_ready, 1)
                pe.wait_ge(qlo_done, n + 1)
                for s in range(SPB):
                    last = mm(S[0][:, s * C:(s + 1) * C], x1f[:, s * TT:(s + 1) * TT], wv_sb[:], start=True, stop=True)
                last.then_inc(v_ready, 1)

            def scores(n, half, u):
                ub = unit_base(n, half)
                s, hg, nk = u // UPS[half], u % UPS[half], TT * (half + 1)
                h0, nh = hg * HG[half], HG[half]
                if u >= 2:
                    pe.wait_ge(exp_done, ub + u - 1)
                elif u == 0:
                    pe.wait_ge(v_done, n + 1)
                    pe.wait_ge(klo_done, n + 1)
                if hg == 0:
                    pe.wait_ge(kbd_in[s % 2], kbd_loaded(n, half, s))
                dst = S[u % 2][:, 0:nh * nk].rearrange("p (h k) -> p h k", k=nk)
                ts = slice(s * TT, (s + 1) * TT)
                keys = [k_bd[:, s % 2, p, h0:h0 + nh, 0:nk] for p in range(2)]
                mm(dst, qhi[:, ts], keys[0], start=True, stop=False)
                mm(dst, qhi[:, ts], keys[1], start=False, stop=False)
                mm(dst, qlo[:, ts], keys[0], start=False, stop=False)
                mm(dst[:, :, nk - TT:nk], idb_sb[:], causal_sb[:, 0:nh, :], start=False, stop=True
                   ).then_inc(scores_ready, 1)

            def probs_t(n, half, u, first=False):
                ub = unit_base(n, half)
                pe.wait_ge(scaled, ub + u + 1)
                if u:
                    pe.wait_ge(pt_done, ub + u)
                elif not first:
                    pe.wait_ge(x2lo_done, n)
                for i in range(HG[half] * (half + 1)):
                    last = nc.tensor.transpose(T[:, i * TT:(i + 1) * TT], p_sb[:, u % 2, i * TT:(i + 1) * TT], id_sb[:])
                last.then_inc(pt_ready, 1)

            def values(n, half, u, first=False):
                ub = unit_base(n, half)
                s, hg = u // UPS[half], u % UPS[half]
                pe.wait_ge(pt_done, ub + u + 1)
                if hg == 0:
                    if s or not first:
                        pe.wait_ge(ot_done, 4 * n + s)
                    if first and s == 0:
                        pe.wait_ge(gates_tanh, 32)
                if half and u == 0:
                    pe.wait_ge(v_back, 16 * (n - HBLK) + 16)
                for kt in range(half + 1):
                    for i in range(HG[half]):
                        h = hg * HG[half] + i
                        v = (v_prev if kt < half else v_cur)[:, s, h, :]
                        c0 = (i * (half + 1) + kt) * TT
                        last = mm(A[VW * (h % 3):VW * (h % 3) + VW, (h // 3) * TT:(h // 3 + 1) * TT], v,
                                  pt_sb[:, u % 2, c0:c0 + TT], start=(kt == 0), stop=(kt == half))
                last.then_inc(av_ready, 1)

            def project_out(n, half, s):
                pe.wait_ge(ot_done, 4 * n + s + 1)
                if half == 0:
                    pe.wait_ge(t_half, 16 + 4 * n + s + 1)
                elif s:
                    pe.wait_ge(t1_done, 4 * n + s)
                else:
                    pe.wait_ge(route_dve, GATE_STEPS * (n - 1) + 1)
                for a in range(2):
                    last = mm(M[:, 0:C], o_t[:, a], wp_sb[:, a], start=(a == 0), stop=(a == 1))
                last.then_inc(proj_ready, 1)

            def expert_out(n, s, part, parts):
                if part == 0:
                    if s < 2:
                        pe.wait_ge(gelu_done, NCH * n + NCH)
                    else:
                        pe.wait_ge(comb, 16 * n + 4 * s - 4)
                    mm(F[s % 2][:, 0:E * C], ones2[:], b2hl[:], start=True, stop=False, skip_group_check=True)
                for c in range(part * NCH // parts, (part + 1) * NCH // parts):
                    e = c // CPE
                    last = mm(F[s % 2][:, e * C:(e + 1) * C], hid[:, c, s * TT:(s + 1) * TT], w2_sb[:, c],
                              start=False, stop=(c == NCH - 1), skip_group_check=True)
                if part == parts - 1:
                    last.then_inc(y_ready, 1)

            def body(n, half, first=False, last=False):
                ups, nu = UPS[half], NU[half]
                ub = unit_base(n, half)
                scores(n, half, 0)
                scores(n, half, 1)
                for j in range(nu):
                    if not first:
                        expert_out(n - 1, j // ups, j % ups, ups)
                    probs_t(n, half, j, first=first)
                    if j + 2 < nu:
                        scores(n, half, j + 2)
                    if j:
                        values(n, half, j - 1, first=first)
                    for s in range(SPB - 1):
                        if j == (s + 1) * ups + 1:
                            project_out(n, half, s)
                    if half == 0 and j % 2 == 0:
                        q = j // 2
                        m = 16 + 4 * n + q
                        gates(m, q % 2, 8 + 2 * n + q // 2, G, 2 * m)
                        if q:
                            pe.wait_ge(t1_done, 4 * n + q - 1) if q > 1 else None
                            skip_in_body(n, q - 1, first)
                values(n, half, nu - 1, first=first)
                if half == 0:
                    skip_in_body(n, 3, first)
                if not last:
                    pe.wait_ge(exp_done, ub + nu)
                    tokens_first(n + 1)
                project_out(n, half, SPB - 1)
                if not last:
                    channels_first(n + 1)
                pe.wait_ge(xh2_done, 4 * n + 4)
                pe.wait_ge(pt_done, ub + nu)
                for s in range(SPB):
                    ins = nc.tensor.transpose(T[0:C, s * TT:(s + 1) * TT], xh2[:, s], id_sb[:])
                ins.then_inc(x2t_ready, 1)
                if not last:
                    project(n + 1)
                pe.wait_ge(x2lo_done, n + 1)
                pe.wait_ge(t1_done, 4 * n + 4)
                split3(M[:], whi[:, 2 * C:], wlo[:, 2 * C:], x2hi[:], x2lo[:]).then_inc(route_ready, 1)
                wait_alone(pe, route_copied, n + 1)
                for s in range(SPB):
                    ins = nc.tensor.transpose(M[:, s * E:(s + 1) * E], gt_sb[:, s * TT:(s + 1) * TT], id_sb[0:E, 0:E])
                ins.then_inc(route_t_ready, 1)
                for c in range(NCH):
                    if c >= 2:
                        pe.wait_ge(gelu_done, NCH * n + c - 1)
                    elif not first:
                        pe.wait_ge(comb, 16 * n - 4 + 4 * c)
                    cs = slice(c * 128, (c + 1) * 128)
                    split3(F[c % 2][:], w1hi[:, cs], w1lo[:, cs], x2hi[:], x2lo[:]).then_inc(hid_ready, 1)

            def skip_in_body(n, q, first):
                if q == 0:
                    if first:
                        pe.wait_ge(t_half, 16)
                    else:
                        pe.wait_ge(route_dve, GATE_STEPS * (n - 1) + 1)
                else:
                    pe.wait_ge(t1_done, 4 * n + q)
                skip(16 + 4 * n + q, q % 2)

            tokens_first(0)
            channels_first(0)
            project(0)
            body(0, 0, first=True)
            with pe.Fori(1, HBLK) as n:
                body(n, 0)
            with pe.Fori(HBLK, NBLK - 1) as n:
                body(n, 1)
            body(NBLK - 1, 1, last=True)
            for s in range(SPB):
                expert_out(NBLK - 1, s, 0, 1)


def kernel(x, L0_conv_w_i2s, L0_conv_w_s2s, L0_conv_w_skip, L0_conv_b_skip, L1_attn_Wq, L1_attn_Wk, L1_attn_Wv,
           L1_attn_Wp, L1_attn_bp, L1_ffn_gate_w, L1_ffn_gate_b, L1_ffn_w1, L1_ffn_b1, L1_ffn_w2, L1_ffn_b2):
    import ml_dtypes
    import numpy as np
    import concourse.bacc as bacc
    from concourse.bass_utils import run_bass_kernel_spmd

    f = np.float32
    bf = ml_dtypes.bfloat16
    GROUP = 3
    a = {}
    xp = np.zeros((C, ROWS, B, PADW), f)
    xp[:, :, :, 1:] = np.asarray(x).transpose(1, 2, 0, 3)
    a["x"] = xp.reshape(C, -1)
    per = FEAT // GROUP
    w = np.asarray(L0_conv_w_i2s)[:, :, 0, 0:2].reshape(GROUP, 4, per, C, 2).transpose(3, 4, 1, 0, 2)
    w = w.reshape(C, 2, 4, FEAT)
    wi = np.zeros((C, 2, 2, GATE_M), f)
    ws_a = np.zeros((GATE_M, 2, GATE_M), f)
    ws_b = np.zeros((FEAT, 2, GATE_M), f)
    s2s = np.asarray(L0_conv_w_s2s)[:, :, 0, :].reshape(4, FEAT, FEAT, 3).transpose(2, 3, 0, 1)
    group = np.arange(C) * GROUP // C
    seen = (np.repeat(np.arange(GROUP), per)[None, :] >= group[:, None]).astype(f)
    wi_mask = np.zeros((C, 2, GATE_M), f)
    for g in range(4):
        c, o = g // 2, 64 * (g % 2)
        wi[:, :, c, o:o + FEAT] = w[:, :, g]
        wi_mask[:, c, o:o + FEAT] = seen
        ws_a[0:FEAT, c, o:o + FEAT] = s2s[:, 0, g]
        ws_a[64:, c, o:o + FEAT] = s2s[:, 1, g]
        ws_b[:, c, o:o + FEAT] = s2s[:, 2, g]
    a["wi"], a["wi_mask"], a["ws_a"], a["ws_b"] = wi, wi_mask, ws_a, ws_b
    a["wk_skip"] = np.asarray(L0_conv_w_skip)[:, :, 0, 0].T
    a["skip_mask"] = (group[None, :] >= (np.arange(FEAT) * GROUP // FEAT)[:, None]).astype(f)
    a["b_skip"] = np.asarray(L0_conv_b_skip).reshape(C, 1)
    a["wq"], a["wk"], a["wv"] = (np.asarray(z).transpose(1, 0, 2).reshape(C, C)
                                 for z in (L1_attn_Wq, L1_attn_Wk, L1_attn_Wv))
    wp = np.zeros((3, VW, 2, C), f)
    wp[:, 0:HS] = np.asarray(L1_attn_Wp).reshape(2, 3, HS, C).transpose(1, 2, 0, 3)
    a["wp"] = wp.reshape(3 * VW, 2, C)
    a["bp"] = np.broadcast_to(np.asarray(L1_attn_bp), (128, C))
    gw = np.zeros((C, 128), f)
    gw[:, 0:E] = np.asarray(L1_ffn_gate_w)
    a["gate_w"] = gw
    a["gate_b"] = np.broadcast_to(np.tile(np.asarray(L1_ffn_gate_b), SPB), (128, SPB * E))
    a["w1"] = np.asarray(L1_ffn_w1).transpose(1, 0, 2).reshape(C, E * HID)
    a["b1"] = np.asarray(L1_ffn_b1).reshape(NCH, 128).T
    a["w2"] = np.asarray(L1_ffn_w2).reshape(NCH, 128, C).transpose(1, 0, 2)
    a["b2"] = np.broadcast_to(np.asarray(L1_ffn_b2).reshape(1, E * C), (2, E * C))
    a["ident"] = np.eye(128, dtype=f)
    a["ident_bf"] = np.eye(128).astype(bf)
    t, k = np.arange(TT)[:, None], np.arange(TT)[None, :]
    masked = np.where(k <= t, 0.0, float(ml_dtypes.finfo(bf).min)).astype(bf)
    a["causal_bf"] = np.broadcast_to(masked[:, None, :], (128, HG[0], TT))
    e, j = np.arange(E)[:, None], np.arange(E)[None, :]
    a["lower"] = np.broadcast_to((j < e).astype(f).reshape(1, E * E), (128, E * E))

    nc = bacc.Bacc("TRN2", target_bir_lowering=False, num_devices=1)
    arrays, args = {}, {}
    for name, v in a.items():
        v = np.ascontiguousarray(v)
        arrays[f"in_{name}"] = v
        args[name] = nc.dram_tensor(f"in_{name}", v.shape, mybir.dt.from_np(v.dtype), kind="ExternalInput").ap()
    args["out"] = nc.dram_tensor("out_y", (NBLK, 128, SPB, C), F32, kind="ExternalOutput").ap()
    hybrid_kernel(nc, **args)
    r = run_bass_kernel_spmd(nc, [arrays], core_ids=[0])
    y = r.results[0]["out_y"].reshape(2, HBLK, 8, W, SPB, C)
    return y.transpose(1, 4, 5, 0, 2, 3).reshape(B, C, ROWS, W)
```

```python
from contextlib import ExitStack

import concourse.bass as bass
from concourse import mybir

F32 = mybir.dt.float32
F32R = mybir.dt.float32r
BF16 = mybir.dt.bfloat16
ALU = mybir.AluOpType
ACT = mybir.ActivationFunctionType
AX = mybir.AxisListType

B, C, ROWS, W = 16, 96, 16, 16
FEAT = 48
PADW = W + 1
HPADW = W + 2
GATE_M = 64 + FEAT
HALF = B // 2
HC = HALF * W
HEADS, HS = 6, 16
VW = 32
TT = 128
SPB = 4
BT = SPB * TT
NBLK = B * ROWS * W // BT
STEPS = 2 * ROWS
E, HID = 4, 384
NCH = E * HID // 128
CPE = HID // 128
SCALE = float(C) ** -0.5
GATE_STEPS = 14

HG = (3, 2)
UNITS = [(a, t, h) for a in range(2) for t in range(2) for h in range(0, HEADS, HG[t])]
NU = len(UNITS)
TILE_END = [1 + max(u for u, (a, t, _) in enumerate(UNITS) if 2 * a + t == s) for s in range(SPB)]
SPREAD = 3
EARLY_T0, EARLY_XT = 1, 5


def hybrid_kernel(nc, x, wi, wi_mask, ws_a, ws_b, wk_skip, skip_mask, b_skip, wq, wk, wv, wp, bp,
                  gate_w, gate_b, w1, b1, w2, b2, ident, ident_bf, causal_bf, lower, out):
    with ExitStack() as ctx:
        def sb(name, shape, dt=F32):
            return ctx.enter_context(nc.sbuf_tensor(name, shape, dt))

        def bank(name):
            return ctx.enter_context(nc.psum_tensor(name, [128, 512], F32))

        def sem(name):
            return ctx.enter_context(nc.semaphore(name))

        id_sb = sb("id_sb", [128, 128])
        idb_sb = sb("idb_sb", [128, 128], BF16)
        causal_sb = sb("causal_sb", [128, HG[0], 128], BF16)
        lower_sb = sb("lower_sb", [128, E * E])
        wi_sb = sb("wi_sb", [C, 2, 2, GATE_M])
        wim_sb = sb("wim_sb", [C, 2, GATE_M])
        wsa_sb = sb("wsa_sb", [GATE_M, 2, GATE_M])
        wsb_sb = sb("wsb_sb", [GATE_M, 2, GATE_M])
        wsk_sb = sb("wsk_sb", [GATE_M, C])
        wskm_sb = sb("wskm_sb", [GATE_M, C])
        bsk_sb = sb("bsk_sb", [C, 1])
        wraw = sb("wraw", [C, 2 * C + 128])
        whi = sb("whi", [C, 2 * C + 128], F32R)
        wlo = sb("wlo", [C, 2 * C + 128], F32R)
        wv_sb = sb("wv_sb", [C, C])
        wp_sb = sb("wp_sb", [C, 2, C])
        bp_sb = sb("bp_sb", [128, C])
        gb_sb = sb("gb_sb", [128, SPB * E])
        w1hi = sb("w1hi", [C, E * HID], F32R)
        w1lo = sb("w1lo", [C, E * HID], F32R)
        b1_sb = sb("b1_sb", [128, NCH])
        w2_sb = sb("w2_sb", [128, NCH, C])
        b2_sb = sb("b2_sb", [2, E * C])
        b2t = sb("b2t", [2, E * C], F32R)
        b2l = sb("b2l", [2, E * C])
        b2p = sb("b2p", [2, E * C])
        b2hl = sb("b2hl", [2, E * C], F32R)
        ones2 = sb("ones2", [2, 128], F32R)
        nhalf = sb("nhalf", [128, SPB])
        x_pad = sb("x_pad", [C, ROWS * B * PADW])
        h_pad = sb("h_pad", [GATE_M, B, HPADW])
        t_ig = sb("t_ig", [FEAT, 2, 2, HC])
        t_fg = sb("t_fg", [FEAT, 2, 2, HC])
        g1 = sb("g1", [FEAT, 2, HC])
        fc = sb("fc", [FEAT, 2, HC])
        ig = sb("ig", [FEAT, 2, HC])
        c4 = sb("c4", [FEAT, 2, HC])
        c2 = sb("c2", [FEAT, 2, HC])
        tc_sb = sb("tc_sb", [FEAT, 2, HC])
        t_cm = sb("t_cm", [C, NBLK * BT])
        t_st = sb("t_st", [C, BT])
        t0 = sb("t0", [128, SPB, C])
        tb = sb("tb", [128, SPB, C])
        st1 = sb("st1", [128, SPB, 6])
        mv1 = sb("mv1", [128, SPB, 2])
        ve1 = sb("ve1", [128, SPB])
        rs1 = sb("rs1", [128, SPB])
        xh = sb("xh", [128, SPB, C])
        x1hi = sb("x1hi", [C, BT], F32R)
        x1lo = sb("x1lo", [C, BT], F32R)
        x1f = sb("x1f", [C, BT])
        qhi = sb("qhi", [C, BT], F32R)
        qlo = sb("qlo", [C, BT], F32R)
        k_cur = sb("k_cur", [C, 2, BT], F32R)
        k_bd = sb("k_bd", [C, 2, 2, HEADS, 2 * TT], F32R)
        v_cur = sb("v_cur", [128, SPB, HEADS, VW])
        nmax = sb("nmax", [128, 2, HG[0]])
        den = sb("den", [128, 2, HG[0]])
        rden = sb("rden", [128, 2, HG[0]])
        p_sb = sb("p_sb", [128, 2, 512])
        pt_sb = sb("pt_sb", [128, 2, 512])
        o_t = sb("o_t", [C, 2, TT])
        t1 = sb("t1", [128, SPB, C])
        t1p = sb("t1p", [128, SPB, C])
        st2 = sb("st2", [128, SPB, 6])
        mv2 = sb("mv2", [128, SPB, 2])
        ve2 = sb("ve2", [128, SPB])
        rs2 = sb("rs2", [128, SPB])
        xh2 = sb("xh2", [128, SPB, C])
        x2hi = sb("x2hi", [C, BT], F32R)
        x2lo = sb("x2lo", [C, BT], F32R)
        gt_sb = sb("gt_sb", [E, BT])
        gl = sb("gl", [128, SPB, E])
        gm = sb("gm", [128, SPB])
        gd = sb("gd", [128, SPB, E])
        ge = sb("ge", [128, SPB, E])
        gtr = sb("gtr", [128, SPB, E, E])
        geq = sb("geq", [128, SPB, E, E])
        geo = sb("geo", [128, SPB, E, E])
        gbt = sb("gbt", [128, SPB, E, E])
        grk = sb("grk", [128, SPB, E])
        gkp = sb("gkp", [128, SPB, E])
        gs = sb("gs", [128, SPB])
        gs2 = sb("gs2", [128, SPB])
        gdn = sb("gdn", [128, SPB])
        grd = sb("grd", [128, SPB])
        gw = sb("gw", [128, SPB, E])
        hid = sb("hid", [128, NCH, BT])
        w1raw = hid[0:C, 0:3, :].rearrange("p a b -> p (a b)")
        y_sb = sb("y_sb", [128, SPB, C])

        M = bank("M")
        A = bank("A")
        S = [bank("S0"), bank("S1")]
        T = bank("T")
        F = [bank("F0"), bank("F1"), bank("F2")]

        gates_ready = sem("gates_ready")
        skip_ready = sem("skip_ready")
        tt_ready = sem("tt_ready")
        xt_ready = sem("xt_ready")
        q_ready = sem("q_ready")
        k_ready = sem("k_ready")
        v_ready = sem("v_ready")
        scores_ready = sem("scores_ready")
        pt_ready = sem("pt_ready")
        av_ready = sem("av_ready")
        proj_ready = sem("proj_ready")
        x2t_ready = sem("x2t_ready")
        route_ready = sem("route_ready")
        route_t_ready = sem("route_t_ready")
        hid_ready = sem("hid_ready")
        y_ready = sem("y_ready")
        gates_tanh = sem("gates_tanh")
        cell_tanh = sem("cell_tanh")
        t0_done = sem("t0_done")
        x1_copied = sem("x1_copied")
        qhi_done = sem("qhi_done")
        khi_done = sem("khi_done")
        v_done = sem("v_done")
        exp_done = sem("exp_done")
        ot_done = sem("ot_done")
        x2hi_done = sem("x2hi_done")
        route_copied = sem("route_copied")
        route_exp = sem("route_exp")
        gelu_done = sem("gelu_done")
        cell_dve = sem("cell_dve")
        h_ready = sem("h_ready")
        t_half = sem("t_half")
        ln1_stats = sem("ln1_stats")
        ln1_aggr = sem("ln1_aggr")
        xh_done = sem("xh_done")
        x1lo_done = sem("x1lo_done")
        qlo_done = sem("qlo_done")
        klo_done = sem("klo_done")
        max_done = sem("max_done")
        rden_done = sem("rden_done")
        pt_done = sem("pt_done")
        t1_done = sem("t1_done")
        ln2_stats = sem("ln2_stats")
        ln2_aggr = sem("ln2_aggr")
        xh2_done = sem("xh2_done")
        x2lo_done = sem("x2lo_done")
        route_dve = sem("route_dve")
        comb = sem("comb")
        scaled = sem("scaled")
        rs1_step = sem("rs1_step")
        rs2_step = sem("rs2_step")
        tb_done = sem("tb_done")
        w_rec_in = sem("w_rec_in")
        x_in = [sem(f"x_in{i}") for i in range(4)]
        w_in = sem("w_in")
        w1_in = sem("w1_in")
        t_staged = sem("t_staged")
        t1p_done = sem("t1p_done")
        kbd_in = [sem("kbd_in0"), sem("kbd_in1")]
        y_out = sem("y_out")
        zeroed = sem("zeroed")
        w_dve = sem("w_dve")
        w_act = sem("w_act")

        N_REC_W = 7
        WSPLIT_ACT = 3
        block = ctx.enter_context(nc.Block())

        def x_row(r0):
            return x_pad[:, bass.ds(r0 * (B * PADW), B * PADW)].rearrange("p (b w) -> p b w", w=PADW)

        KBD = HEADS * 16

        def out_parts(slot):
            todo = SPREAD * NCH
            return [divmod(i, NCH) for i in range(todo * slot // NU, todo * (slot + 1) // NU)]

        def wait_alone(eng, semaphore, value):
            if not isinstance(value, int):
                value = eng.snap(eng.to_reg(value))
            eng.wait_ge(zeroed, 5)
            eng.wait_ge(semaphore, value)

        def as_f32(ap):
            return ap.bitcast(F32)

        @block.sync
        def _(sp):
            for dst, src in ((wi_sb, wi), (wim_sb, wi_mask), (wsa_sb, ws_a), (wsb_sb, ws_b),
                             (wsk_sb, wk_skip), (wskm_sb, skip_mask), (bsk_sb, b_skip)):
                sp.dma_start(dst[:], src).then_inc(w_rec_in, 16)
            rows = ROWS * B * PADW // 4
            for i in range(4):
                sp.dma_start(x_pad[:, i * rows:(i + 1) * rows], x[:, i * rows:(i + 1) * rows]).then_inc(x_in[i], 16)
                if i == 0:
                    for dst, src in ((id_sb[:], ident), (idb_sb[:], ident_bf), (causal_sb[:], causal_bf),
                                     (lower_sb[:], lower), (wraw[:, 0:C], wq), (wraw[:, C:2 * C], wk),
                                     (wraw[:, 2 * C:], gate_w), (wv_sb[:], wv), (wp_sb[:], wp), (bp_sb[:], bp),
                                     (gb_sb[:], gate_b), (b1_sb[:], b1), (b2_sb[:], b2), (w2_sb[:], w2)):
                        sp.dma_start(dst, src).then_inc(w_in, 16)
                    sp.dma_start(w1raw, w1).then_inc(w1_in, 16)

            def stage(n):
                sp.dma_start(t_st[:], t_cm[:, bass.ds(n * BT, BT)]).then_inc(t_staged, 16)

            def load_keys(a):
                for h in range(HEADS):
                    rows_h = slice(h * HS, (h + 1) * HS)
                    sp.dma_start(as_f32(k_bd[rows_h, a, :, h, :]),
                                 as_f32(k_cur[rows_h, :, a * 2 * TT:(a + 1) * 2 * TT])).then_inc(kbd_in[a], 16)

            def body(n, first=False, last=False):
                wait_alone(sp, klo_done, n + 1)
                if not first:
                    wait_alone(sp, scores_ready, NU * n)
                load_keys(0)
                load_keys(1)
                if not last:
                    wait_alone(sp, tt_ready, n + 1)
                    stage(n + 1)
                if not first:
                    store_y(n - 1)

            def store_y(n):
                wait_alone(sp, comb, 16 * n + 16)
                sp.dma_start(out[bass.ds(n, 1)].rearrange("a p s c -> p (a s) c"), y_sb[:]).then_inc(y_out, 16)

            sp.wait_ge(zeroed, 5)
            sp.wait_ge(t_half, STEPS)
            stage(0)
            body(0, first=True)
            with sp.Fori(1, NBLK - 1) as n:
                body(n)
            body(NBLK - 1, last=True)
            store_y(NBLK - 1)
            sp.wait_ge(y_out, 16 * NBLK)

        @block.gpsimd
        def _(pool):
            nc.gpsimd.memset(h_pad[:], 0.0).then_inc(zeroed, 1)
            nc.gpsimd.memset(c2[:], 0.0).then_inc(zeroed, 1)
            nc.gpsimd.memset(as_f32(k_bd[:]), 0.0).then_inc(zeroed, 1)
            nc.gpsimd.memset(v_cur[:], 0.0).then_inc(zeroed, 1)
            nc.gpsimd.memset(nhalf[:], -0.5).then_inc(zeroed, 1)
            pool.wait_ge(zeroed, 5)

            def rstd1(n):
                wait_alone(pool, ln1_aggr, 4 * n + 4)
                nc.gpsimd.tensor_scalar(ve1[:], mv1[:, :, 1], 1e-5, None, ALU.add).then_inc(rs1_step, 1)
                pool.wait_ge(rs1_step, 2 * n + 1)
                nc.gpsimd.tensor_tensor(rs1[:], ve1[:], nhalf[:], ALU.pow).then_inc(rs1_step, 1)

            def rstd2(n, s):
                wait_alone(pool, ln2_aggr, 4 * n + s + 1)
                nc.gpsimd.tensor_scalar(ve2[:, s:s + 1], mv2[:, s, 1:2], 1e-5, None, ALU.add).then_inc(rs2_step, 1)
                pool.wait_ge(rs2_step, 8 * n + 2 * s + 1)
                nc.gpsimd.tensor_tensor(rs2[:, s:s + 1], ve2[:, s:s + 1], nhalf[:, 0:1], ALU.pow).then_inc(rs2_step, 1)

            def residual(n):
                pool.wait_ge(t0_done, n + 1)
                nc.gpsimd.tensor_tensor(tb[:], t0[:], bp_sb[:].unsqueeze(1).to_broadcast((128, SPB, C)),
                                        ALU.add).then_inc(tb_done, 1)

            def scale(n, u):
                wait_alone(pool, rden_done, NU * n + u + 1)
                _, t, _ = UNITS[u]
                nk = TT * (t + 1)
                for i in range(HG[t]):
                    p = p_sb[:, u % 2, i * nk:(i + 1) * nk]
                    last = nc.gpsimd.tensor_scalar(p, p, rden[:, u % 2, i:i + 1], 1.0, ALU.mult, ALU.mult)
                last.then_inc(scaled, 1)

            def body(n, last=False):
                scale(n, 0)
                for j in range(NU):
                    if j + 1 < NU:
                        scale(n, j + 1)
                    if j == EARLY_T0 + 1 and not last:
                        rstd1(n + 1)
                    for s in range(SPB - 1):
                        if j == TILE_END[s] + 1:
                            rstd2(n, s)
                rstd2(n, SPB - 1)
                if not last:
                    pool.wait_ge(t1_done, 4 * n + 4)
                    residual(n + 1)

            pool.wait_ge(w_in, 16 * 14)
            rstd1(0)
            residual(0)
            with pool.Fori(0, NBLK - 1) as n:
                body(n)
            body(NBLK - 1, last=True)

        @block.scalar
        def _(act):
            def cell_gates(m, hb, src):
                act.wait_ge(gates_ready, m + 1)
                v = src[:, 0:2 * HC].rearrange("p (c n) -> p c n", c=2)
                nc.scalar.activation(t_fg[:, hb], v[64:64 + FEAT], ACT.Tanh, scale=0.5).then_inc(gates_tanh, 1)
                nc.scalar.activation(t_ig[:, hb], v[0:FEAT], ACT.Tanh, scale=0.5).then_inc(gates_tanh, 1)

            def cell_out(m, hb):
                act.wait_ge(cell_dve, 5 * m + 4)
                nc.scalar.activation(tc_sb[:, hb], c4[:, hb], ACT.Tanh, scale=0.25).then_inc(cell_tanh, 1)

            def rec0(it):
                for q in range(4):
                    m = 4 * it + q
                    cell_gates(m, q % 2, (F[2], A)[q % 2])
                    cell_out(m, q % 2)

            act.wait_ge(w_in, 16 * 14)
            nc.scalar.copy(whi[:], wraw[:]).then_inc(w_act, 1)
            nc.scalar.copy(b2t[:], b2_sb[:]).then_inc(w_act, 1)
            act.wait_ge(w1_in, 16)
            nc.scalar.copy(w1hi[:], w1raw).then_inc(w_act, 1)
            with act.Fori(0, ROWS // 2) as it:
                rec0(it)

            def take_t0(n, first=False):
                act.wait_ge(tt_ready, n + 1)
                if not first:
                    act.wait_ge(tb_done, n)
                nc.scalar.copy(t0[:], M[:, 0:SPB * C].rearrange("p (s c) -> p s c", s=SPB)).then_inc(t0_done, 1)

            def take_x1(n):
                act.wait_ge(xt_ready, n + 1)
                nc.scalar.copy(x1hi[:], M[0:C, :]).then_inc(x1_copied, 1)
                nc.scalar.copy(x1f[:], M[0:C, :]).then_inc(x1_copied, 1)

            def take_qk(n):
                act.wait_ge(q_ready, n + 1)
                nc.scalar.mul(qhi[:], S[0][0:C, :], SCALE).then_inc(qhi_done, 1)
                act.wait_ge(k_ready, n + 1)
                nc.scalar.copy(k_cur[:, 0, :], S[1][0:C, :]).then_inc(khi_done, 1)

            def take_v(n):
                act.wait_ge(v_ready, n + 1)
                nc.scalar.copy(v_cur[:, :, :, 0:HS],
                               S[0][:, 0:SPB * C].rearrange("p (s h d) -> p s h d", s=SPB, h=HEADS)).then_inc(v_done, 1)

            def exps(n, u, first=False):
                act.wait_ge(max_done, NU * n + u + 1)
                if u >= 2 or not first:
                    act.wait_ge(pt_ready, NU * n + u - 1)
                _, t, _ = UNITS[u]
                nk = TT * (t + 1)
                for i in range(HG[t]):
                    last = nc.scalar.activation(p_sb[:, u % 2, i * nk:(i + 1) * nk], S[u % 2][:, i * nk:(i + 1) * nk],
                                                ACT.Exp, bias=nmax[:, u % 2, i:i + 1],
                                                accum_out=den[:, u % 2, i:i + 1])
                last.then_inc(exp_done, 1)

            def heads_out(n, s, first=False):
                act.wait_ge(av_ready, NU * n + TILE_END[s])
                if s or not first:
                    act.wait_ge(proj_ready, 4 * n + s)
                nc.scalar.copy(o_t[:], A[0:C, 0:2 * TT].rearrange("p (a t) -> p a t", a=2)).then_inc(ot_done, 1)

            def body(n, first=False, last=False):
                if not first:
                    act.wait_ge(route_dve, GATE_STEPS * (n - 1) + 3)
                    nc.scalar.activation(ge[:], gd[:], ACT.Exp).then_inc(route_exp, 1)
                exps(n, 0, first)
                for j in range(NU):
                    if j + 1 < NU:
                        exps(n, j + 1, first)
                    for s in range(SPB - 1):
                        if j == TILE_END[s]:
                            heads_out(n, s, first)
                    if j == EARLY_T0 and not last:
                        take_t0(n + 1)
                    if j == EARLY_XT and not last:
                        take_x1(n + 1)
                heads_out(n, SPB - 1, first)
                if not last:
                    act.wait_ge(kbd_in[0], KBD * (n + 1))
                    act.wait_ge(kbd_in[1], KBD * (n + 1))
                    take_qk(n + 1)
                act.wait_ge(x2t_ready, n + 1)
                nc.scalar.copy(x2hi[:], T[0:C, :]).then_inc(x2hi_done, 1)
                if not last:
                    take_v(n + 1)
                if not first:
                    act.wait_ge(y_ready, 4 * n)
                for c in range(NCH):
                    act.wait_ge(hid_ready, NCH * n + c + 1)
                    nc.scalar.activation(hid[:, c, :], F[(c + 1) % 3][:], ACT.Gelu, bias=b1_sb[:, c:c + 1]
                                         ).then_inc(gelu_done, 1)
                    if c == 3:
                        act.wait_ge(route_ready, n + 1)
                        nc.scalar.copy(gt_sb[:], M[0:E, :]).then_inc(route_copied, 1)
                act.wait_ge(t1_done, 4 * n + 4)
                if not first:
                    act.wait_ge(comb, 16 * n)
                nc.scalar.copy(t1p[:], t1[:]).then_inc(t1p_done, 1)

            take_t0(0, first=True)
            take_x1(0)
            take_qk(0)
            take_v(0)
            body(0, first=True)
            with act.Fori(1, NBLK - 1) as n:
                body(n)
            body(NBLK - 1, last=True)
            act.wait_ge(route_dve, GATE_STEPS * (NBLK - 1) + 3)
            nc.scalar.activation(ge[:], gd[:], ACT.Exp).then_inc(route_exp, 1)

        @block.vector
        def _(dve):
            V = nc.vector
            steps = [0]

            def setup_step(ins):
                steps[0] += 1
                ins.then_inc(w_dve, 1)

            dve.wait_ge(w_rec_in, 16 * N_REC_W)
            setup_step(V.tensor_tensor(wi_sb[:, 1], wi_sb[:, 1], wim_sb[:], ALU.mult))
            setup_step(V.tensor_scalar(wsa_sb[:], wsa_sb[:], 0.5, None, ALU.mult))
            setup_step(V.tensor_scalar(wsb_sb[:], wsb_sb[:], 0.5, None, ALU.mult))
            setup_step(V.scalar_tensor_tensor(wsk_sb[:], wsk_sb[:], 0.5, wskm_sb[:], ALU.mult, ALU.mult))
            setup_step(V.memset(as_f32(ones2[:]), 1.0))
            dve.wait_ge(w_act, WSPLIT_ACT)
            setup_step(V.tensor_tensor(wlo[:], wraw[:], as_f32(whi[:]), ALU.subtract))
            setup_step(V.tensor_tensor(w1lo[:], w1raw, as_f32(w1hi[:]), ALU.subtract))
            setup_step(V.tensor_tensor(b2l[:], b2_sb[:], as_f32(b2t[:]), ALU.subtract))
            setup_step(V.tensor_scalar(b2p[:], as_f32(b2t[:]), id_sb[0:2, 0:1], None, ALU.mult))
            dve.wait_ge(w_dve, 9)
            setup_step(V.scalar_tensor_tensor(b2hl[:], b2l[:], id_sb[0:2, 1:2], b2p[:], ALU.mult, ALU.add))
            dve.wait_ge(zeroed, 5)

            def cell(m, hb):
                dve.wait_ge(gates_tanh, 2 * m + 1)
                V.tensor_scalar(g1[:, hb], t_fg[:, hb, 1], 1.0, None, ALU.add).then_inc(cell_dve, 1)
                V.scalar_tensor_tensor(fc[:, hb], t_fg[:, hb, 0], 1.0, c2[:, hb], ALU.add, ALU.mult).then_inc(cell_dve, 1)
                dve.wait_ge(gates_tanh, 2 * m + 2)
                dve.wait_ge(cell_dve, 5 * m + 1)
                V.scalar_tensor_tensor(ig[:, hb], t_ig[:, hb, 1], 1.0, g1[:, hb], ALU.add, ALU.mult).then_inc(cell_dve, 1)
                dve.wait_ge(cell_dve, 5 * m + 3)
                V.tensor_tensor(c4[:, hb], fc[:, hb], ig[:, hb], ALU.add).then_inc(cell_dve, 1)
                dve.wait_ge(cell_dve, 5 * m + 4)
                V.tensor_scalar(c2[:, hb], c4[:, hb], 0.5, None, ALU.mult).then_inc(cell_dve, 1)

            def cell_h(m, hb, first=False):
                dve.wait_ge(cell_tanh, m + 1)
                if not first:
                    dve.wait_ge(skip_ready, m - 1)
                o = t_ig[:, hb, 0].rearrange("p (b w) -> p b w", w=W)
                t = tc_sb[:, hb].rearrange("p (b w) -> p b w", w=W)
                bs = slice(hb * HALF, (hb + 1) * HALF)
                V.scalar_tensor_tensor(h_pad[0:FEAT, bs, 1:1 + W], o, 1.0, t, ALU.add, ALU.mult).then_inc(h_ready, 1)
                V.scalar_tensor_tensor(h_pad[64:64 + FEAT, bs, 0:W], o, 1.0, t, ALU.add, ALU.mult).then_inc(h_ready, 1)

            def add_skip(m, hb, row):
                dve.wait_ge(skip_ready, m + 1)
                bs = slice(hb * HALF, (hb + 1) * HALF)
                dst = t_cm[:].rearrange("p (b t) -> p b t", t=ROWS * W)[:, bs, bass.ds(row * W, W)]
                V.scalar_tensor_tensor(dst, M[0:C, hb * HC:(hb + 1) * HC].rearrange("p (b w) -> p b w", w=W),
                                       bsk_sb[:, 0:1], x_row(row)[:, bs, 1:], ALU.add, ALU.add).then_inc(t_half, 1)

            def rec0(it, first):
                for q in range(4):
                    m, hb = 4 * it + q, q % 2
                    cell(m, hb)
                    cell_h(m, hb, first=first and q < 2)
                    if q >= 2 or not first:
                        add_skip(m - 2, hb, 2 * it + q // 2 - 1)

            dve.wait_ge(x_in[0], 16)
            rec0(0, True)
            for i in (1, 2, 3):
                dve.wait_ge(x_in[i], 16)
            with dve.Fori(1, ROWS // 2) as it:
                rec0(it, False)
            for hb in range(2):
                add_skip(STEPS - 2 + hb, hb, ROWS - 1)

            def norm1(n):
                dve.wait_ge(t0_done, n + 1)
                for s in range(SPB):
                    V.bn_stats(st1[:, s], t0[:, s]).then_inc(ln1_stats, 1)
                wait_alone(dve, ln1_stats, 4 * n + 4)
                for s in range(SPB):
                    V.bn_aggr(mv1[:, s], st1[:, s]).then_inc(ln1_aggr, 1)

            def normalize1(n):
                dve.wait_ge(rs1_step, 2 * n + 2)
                for s in range(SPB):
                    V.tensor_scalar(xh[:, s], t0[:, s], mv1[:, s, 0:1], rs1[:, s:s + 1],
                                    ALU.subtract, ALU.mult).then_inc(xh_done, 1)

            def x1_rest(n):
                dve.wait_ge(x1_copied, 2 * n + 2)
                V.tensor_tensor(x1lo[:], M[0:C, :], as_f32(x1hi[:]), ALU.subtract).then_inc(x1lo_done, 1)

            def q_rest(n):
                dve.wait_ge(qhi_done, n + 1)
                V.scalar_tensor_tensor(qlo[:], S[0][0:C, :], SCALE, as_f32(qhi[:]), ALU.mult, ALU.subtract
                                       ).then_inc(qlo_done, 1)

            def k_rest(n):
                dve.wait_ge(khi_done, n + 1)
                V.tensor_tensor(k_cur[:, 1, :], S[1][0:C, :], as_f32(k_cur[:, 0, :]), ALU.subtract
                                ).then_inc(klo_done, 1)

            def row_max(n, u):
                _, t, _ = UNITS[u]
                nk = TT * (t + 1)
                dve.wait_ge(scores_ready, NU * n + u + 1)
                V.tensor_reduce(nmax[:, u % 2, 0:HG[t]], S[u % 2][:, 0:HG[t] * nk].rearrange("p (h k) -> p h k", k=nk),
                                AX.X, ALU.max, negate=True).then_inc(max_done, 1)

            def recip(n, u):
                dve.wait_ge(exp_done, NU * n + u + 1)
                hg = HG[UNITS[u][1]]
                V.reciprocal(rden[:, u % 2, 0:hg], den[:, u % 2, 0:hg]).then_inc(rden_done, 1)

            def take_pt(n, u, first=False):
                t = UNITS[u][1]
                w = HG[t] * (t + 1) * TT
                dve.wait_ge(pt_ready, NU * n + u + 1)
                if u >= 2 or not first:
                    dve.wait_ge(av_ready, NU * n + u - 1)
                V.tensor_copy(pt_sb[:, u % 2, 0:w], T[:, 0:w]).then_inc(pt_done, 1)

            def attn_residual(n, s, first=False):
                dve.wait_ge(proj_ready, 4 * n + s + 1)
                dve.wait_ge(tb_done, n + 1)
                if s == 0 and not first:
                    dve.wait_ge(t1p_done, n)
                V.tensor_tensor(t1[:, s], M[:, 0:C], tb[:, s], ALU.add).then_inc(t1_done, 1)
                dve.wait_ge(t1_done, 4 * n + s + 1)
                V.bn_stats(st2[:, s], t1[:, s]).then_inc(ln2_stats, 1)
                wait_alone(dve, ln2_stats, 4 * n + s + 1)
                V.bn_aggr(mv2[:, s], st2[:, s]).then_inc(ln2_aggr, 1)

            def normalize2(n, s):
                dve.wait_ge(rs2_step, 8 * n + 2 * s + 2)
                V.tensor_scalar(xh2[:, s], t1[:, s], mv2[:, s, 0:1], rs2[:, s:s + 1],
                                ALU.subtract, ALU.mult).then_inc(xh2_done, 1)

            def route(n, part):
                base = GATE_STEPS * n
                ej = (128, SPB, E, E)
                of_j = ge[:].unsqueeze(2).to_broadcast(ej)
                of_e = ge[:].unsqueeze(3).to_broadcast(ej)
                if part == 0:
                    dve.wait_ge(route_t_ready, n + 1)
                    V.tensor_tensor(gl[:].rearrange("p s e -> p (s e)"), M[:, 0:SPB * E], gb_sb[:], ALU.add
                                    ).then_inc(route_dve, 1)
                    dve.wait_ge(route_dve, base + 1)
                    V.tensor_reduce(gm[:], gl[:], AX.X, ALU.max).then_inc(route_dve, 1)
                    dve.wait_ge(route_dve, base + 2)
                    V.tensor_tensor(gd[:], gl[:], gm[:].unsqueeze(2).to_broadcast((128, SPB, E)), ALU.subtract
                                    ).then_inc(route_dve, 1)
                    return
                dve.wait_ge(route_exp, n + 1)
                V.tensor_tensor(gtr[:], of_j, of_e, ALU.is_gt).then_inc(route_dve, 1)
                V.tensor_tensor(geq[:], of_j, of_e, ALU.is_equal).then_inc(route_dve, 1)
                dve.wait_ge(route_dve, base + 5)
                V.tensor_tensor(geo[:].rearrange("p s e j -> p s (e j)"), geq[:].rearrange("p s e j -> p s (e j)"),
                                lower_sb[:].unsqueeze(1).to_broadcast((128, SPB, E * E)), ALU.mult).then_inc(route_dve, 1)
                dve.wait_ge(route_dve, base + 6)
                V.tensor_tensor(gbt[:], gtr[:], geo[:], ALU.add).then_inc(route_dve, 1)
                dve.wait_ge(route_dve, base + 7)
                V.tensor_reduce(grk[:], gbt[:], AX.X, ALU.add).then_inc(route_dve, 1)
                dve.wait_ge(route_dve, base + 8)
                V.scalar_tensor_tensor(gkp[:], grk[:], 1.5, ge[:], ALU.is_lt, ALU.mult).then_inc(route_dve, 1)
                V.tensor_reduce(gs[:], ge[:], AX.X, ALU.add).then_inc(route_dve, 1)
                dve.wait_ge(route_dve, base + 10)
                V.tensor_reduce(gs2[:], gkp[:], AX.X, ALU.add).then_inc(route_dve, 1)
                dve.wait_ge(route_dve, base + 11)
                V.scalar_tensor_tensor(gdn[:], gs[:], 1e-9, gs2[:], ALU.mult, ALU.add).then_inc(route_dve, 1)
                dve.wait_ge(route_dve, base + 12)
                V.reciprocal(grd[:], gdn[:]).then_inc(route_dve, 1)
                dve.wait_ge(route_dve, base + 13)
                V.tensor_tensor(gw[:], gkp[:], grd[:].unsqueeze(2).to_broadcast((128, SPB, E)), ALU.mult
                                ).then_inc(route_dve, 1)
                dve.wait_ge(route_dve, base + 14)

            def combine(n, s, first):
                dve.wait_ge(y_ready, 4 * n + s + 1)
                dve.wait_ge(t1p_done, n + 1)
                if s == 0 and not first:
                    dve.wait_ge(y_out, 16 * n)
                for e in range(E):
                    if e:
                        dve.wait_ge(comb, 16 * n + 4 * s + e)
                    V.scalar_tensor_tensor(y_sb[:, s], F[s % 3][:, e * C:(e + 1) * C], gw[:, s, e:e + 1],
                                           t1p[:, s] if e == 0 else y_sb[:, s], ALU.mult, ALU.add).then_inc(comb, 1)

            def body(n, first=False, second=False, last=False):
                row_max(n, 0)
                row_max(n, 1)
                recip(n, 0)
                if not first:
                    route(n - 1, 1)
                for j in range(NU):
                    if j + 1 < NU:
                        recip(n, j + 1)
                    take_pt(n, j, first)
                    if j + 2 < NU:
                        row_max(n, j + 2)
                    if not first and j:
                        for s, c in out_parts(j - 1):
                            if c == NCH - 1:
                                combine(n - 1, s, second)
                    if not last:
                        if j == EARLY_T0 + 1:
                            norm1(n + 1)
                        if j == EARLY_T0 + 2:
                            normalize1(n + 1)
                        if j == EARLY_XT:
                            x1_rest(n + 1)
                    for s in range(SPB - 1):
                        if j == TILE_END[s] + 1:
                            attn_residual(n, s, first)
                        if j == TILE_END[s] + 2:
                            normalize2(n, s)
                if not last:
                    q_rest(n + 1)
                attn_residual(n, SPB - 1)
                for s in range(SPB - 1):
                    if TILE_END[s] + 2 >= NU:
                        normalize2(n, s)
                if not last:
                    k_rest(n + 1)
                normalize2(n, SPB - 1)
                if not first:
                    combine(n - 1, SPREAD - 1, second)
                dve.wait_ge(x2hi_done, n + 1)
                V.tensor_tensor(x2lo[:], T[0:C, :], as_f32(x2hi[:]), ALU.subtract).then_inc(x2lo_done, 1)
                if not first:
                    combine(n - 1, SPB - 1, second)
                route(n, 0)

            norm1(0)
            normalize1(0)
            x1_rest(0)
            q_rest(0)
            k_rest(0)
            body(0, first=True)
            body(1, second=True)
            with dve.Fori(2, NBLK - 1) as n:
                body(n)
            body(NBLK - 1, last=True)
            route(NBLK - 1, 1)
            for s in range(SPB):
                combine(NBLK - 1, s, False)

        @block.tensor
        def _(pe):
            mm = nc.tensor.matmul

            def split3(dst, hi_l, lo_l, hi_r, lo_r, stop=True, **kw):
                mm(dst, hi_l, hi_r, start=True, stop=False, **kw)
                mm(dst, hi_l, lo_r, start=False, stop=False, **kw)
                return mm(dst, lo_l, hi_r, start=False, stop=stop, **kw)

            def gates(m, hb, row, dst, free, first=False):
                bs = slice(hb * HALF, (hb + 1) * HALF)
                if free is not None:
                    pe.wait_ge(gates_tanh, free)
                xr = x_row(row)
                for c in range(2):
                    for tap in range(2):
                        last = mm(dst[0:GATE_M, c * HC:(c + 1) * HC], wi_sb[:, tap, c], xr[:, bs, tap:tap + W],
                                  start=(c == 0 and tap == 0), stop=False, skip_group_check=True)
                if not first:
                    pe.wait_ge(h_ready, 2 * m - 2)
                for c in range(2):
                    d = dst[0:GATE_M, c * HC:(c + 1) * HC]
                    mm(d, wsa_sb[:, c], h_pad[:, bs, 0:W], start=False, stop=False, skip_group_check=True)
                    last = mm(d, wsb_sb[:, c], h_pad[:, bs, 2:2 + W], start=False, stop=True, skip_group_check=True)
                last.then_inc(gates_ready, 1)

            def skip(m, hb):
                pe.wait_ge(h_ready, 2 * m + 2)
                bs = slice(hb * HALF, (hb + 1) * HALF)
                mm(M[0:C, hb * HC:(hb + 1) * HC], wsk_sb[:], h_pad[:, bs, 1:1 + W], start=True, stop=True
                   ).then_inc(skip_ready, 1)

            def rec0(it, first):
                for q in range(4):
                    m, hb = 4 * it + q, q % 2
                    started = q >= 2 or not first
                    gates(m, hb, 2 * it + q // 2, (F[2], A)[hb], 2 * m - 2 if started else None, first=not started)
                    if started:
                        if q >= 3 or not first:
                            pe.wait_ge(t_half, m - 2)
                        skip(m - 2, hb)

            pe.wait_ge(w_dve, 4)
            pe.wait_ge(zeroed, 5)
            pe.wait_ge(x_in[0], 16)
            rec0(0, True)
            for i in (1, 2, 3):
                pe.wait_ge(x_in[i], 16)
            with pe.Fori(1, ROWS // 2) as it:
                rec0(it, False)
            for hb in range(2):
                pe.wait_ge(t_half, STEPS - 2 + hb)
                skip(STEPS - 2 + hb, hb)
            pe.wait_ge(w_dve, 10)
            pe.wait_ge(w_in, 16 * 14)

            def tokens_first(n):
                pe.wait_ge(t_staged, 16 * n + 16)
                for s in range(SPB):
                    last = nc.tensor.transpose(M[:, s * C:(s + 1) * C], t_st[:, s * TT:(s + 1) * TT], id_sb[0:C, 0:C])
                last.then_inc(tt_ready, 1)

            def channels_first(n):
                pe.wait_ge(xh_done, 4 * n + 4)
                for s in range(SPB):
                    last = nc.tensor.transpose(M[0:C, s * TT:(s + 1) * TT], xh[:, s], id_sb[:])
                last.then_inc(xt_ready, 1)

            def project_q(n):
                pe.wait_ge(x1lo_done, n + 1)
                split3(S[0][0:C, :], whi[:, 0:C], wlo[:, 0:C], x1hi[:], x1lo[:]).then_inc(q_ready, 1)

            def project_k(n):
                split3(S[1][0:C, :], whi[:, C:2 * C], wlo[:, C:2 * C], x1hi[:], x1lo[:]).then_inc(k_ready, 1)

            def project_v(n):
                pe.wait_ge(qlo_done, n + 1)
                for s in range(SPB):
                    last = mm(S[0][:, s * C:(s + 1) * C], x1f[:, s * TT:(s + 1) * TT], wv_sb[:], start=True, stop=True)
                last.then_inc(v_ready, 1)

            def scores(n, u):
                a, t, h0 = UNITS[u]
                nh, nk, s = HG[t], TT * (t + 1), 2 * a + t
                if u >= 2:
                    pe.wait_ge(exp_done, NU * n + u - 1)
                elif u == 0:
                    pe.wait_ge(v_done, n + 1)
                    pe.wait_ge(klo_done, n + 1)
                if t == 0 and h0 == 0:
                    pe.wait_ge(kbd_in[a], KBD * (n + 1))
                dst = S[u % 2][:, 0:nh * nk].rearrange("p (h k) -> p h k", k=nk)
                ts = slice(s * TT, (s + 1) * TT)
                keys = [k_bd[:, a, p, h0:h0 + nh, 0:nk] for p in range(2)]
                mm(dst, qhi[:, ts], keys[0], start=True, stop=False)
                mm(dst, qhi[:, ts], keys[1], start=False, stop=False)
                mm(dst, qlo[:, ts], keys[0], start=False, stop=False)
                mm(dst[:, :, nk - TT:nk], idb_sb[:], causal_sb[:, 0:nh, :], start=False, stop=True
                   ).then_inc(scores_ready, 1)

            def probs_t(n, u, first=False):
                pe.wait_ge(scaled, NU * n + u + 1)
                if u:
                    pe.wait_ge(pt_done, NU * n + u)
                elif not first:
                    pe.wait_ge(x2lo_done, n)
                t = UNITS[u][1]
                for i in range(HG[t] * (t + 1)):
                    last = nc.tensor.transpose(T[:, i * TT:(i + 1) * TT], p_sb[:, u % 2, i * TT:(i + 1) * TT], id_sb[:])
                last.then_inc(pt_ready, 1)

            def values(n, u, first=False):
                a, t, h0 = UNITS[u]
                s = 2 * a + t
                pe.wait_ge(pt_done, NU * n + u + 1)
                if h0 == 0:
                    if s or not first:
                        pe.wait_ge(ot_done, 4 * n + s)
                for kt in range(t + 1):
                    for i in range(HG[t]):
                        h = h0 + i
                        c0 = (i * (t + 1) + kt) * TT
                        last = mm(A[VW * (h % 3):VW * (h % 3) + VW, (h // 3) * TT:(h // 3 + 1) * TT],
                                  v_cur[:, 2 * a + kt, h, :], pt_sb[:, u % 2, c0:c0 + TT],
                                  start=(kt == 0), stop=(kt == t))
                last.then_inc(av_ready, 1)

            def project_out(n, s):
                pe.wait_ge(ot_done, 4 * n + s + 1)
                for a in range(2):
                    last = mm(M[:, 0:C], o_t[:, a], wp_sb[:, a], start=(a == 0), stop=(a == 1))
                last.then_inc(proj_ready, 1)

            def expert_out(n, parts):
                for s, c in parts:
                    dst = F[s % 3]
                    if c == 0:
                        if s < 3:
                            pe.wait_ge(gelu_done, NCH * n + NCH)
                        else:
                            pe.wait_ge(comb, 16 * n + 4 * (s - 2))
                        mm(dst[:, 0:E * C], ones2[:], b2hl[:], start=True, stop=False, skip_group_check=True)
                    e = c // CPE
                    last = mm(dst[:, e * C:(e + 1) * C], hid[:, c, s * TT:(s + 1) * TT], w2_sb[:, c],
                              start=False, stop=(c == NCH - 1), skip_group_check=True)
                    if c == NCH - 1:
                        last.then_inc(y_ready, 1)

            def expert_hidden(n, chunks, first):
                for c in chunks:
                    if c >= 3:
                        pe.wait_ge(gelu_done, NCH * n + c - 2)
                    elif not first:
                        pe.wait_ge(comb, 16 * n - 16 + 4 * (c + 2))
                    cs = slice(c * 128, (c + 1) * 128)
                    split3(F[(c + 1) % 3][:], w1hi[:, cs], w1lo[:, cs], x2hi[:], x2lo[:]).then_inc(hid_ready, 1)

            def body(n, first=False, last=False):
                tail = [(SPB - 1, c) for c in range(NCH)]
                scores(n, 0)
                scores(n, 1)
                for j in range(NU):
                    if not first:
                        expert_out(n - 1, out_parts(j))
                    probs_t(n, j, first)
                    if j + 2 < NU:
                        scores(n, j + 2)
                    if j:
                        values(n, j - 1, first)
                    if j == EARLY_T0 and not last:
                        if first:
                            pe.wait_ge(x1lo_done, n + 1)
                        else:
                            pe.wait_ge(route_dve, GATE_STEPS * (n - 1) + 1)
                        tokens_first(n + 1)
                    if j == EARLY_XT and not last:
                        pe.wait_ge(t1_done, 4 * n + 1)
                        channels_first(n + 1)
                    for s in range(SPB - 1):
                        if j == TILE_END[s] + 1:
                            if last:
                                if s:
                                    pe.wait_ge(t1_done, 4 * n + s)
                                else:
                                    pe.wait_ge(route_dve, GATE_STEPS * (n - 1) + 1)
                            elif s == 0:
                                pe.wait_ge(t0_done, n + 2)
                            elif s == 1:
                                pe.wait_ge(x1lo_done, n + 2)
                            else:
                                pe.wait_ge(t1_done, 4 * n + s)
                            project_out(n, s)
                values(n, NU - 1, first)
                if not last:
                    pe.wait_ge(exp_done, NU * n + NU)
                    project_q(n + 1)
                pe.wait_ge(t1_done, 4 * n + 3)
                project_out(n, SPB - 1)
                if not last:
                    project_k(n + 1)
                if not first:
                    expert_out(n - 1, tail[0:NCH // 2])
                pe.wait_ge(xh2_done, 4 * n + 4)
                pe.wait_ge(pt_done, NU * n + NU)
                for s in range(SPB):
                    ins = nc.tensor.transpose(T[0:C, s * TT:(s + 1) * TT], xh2[:, s], id_sb[:])
                ins.then_inc(x2t_ready, 1)
                if not first:
                    expert_out(n - 1, tail[NCH // 2:])
                if not last:
                    project_v(n + 1)
                pe.wait_ge(x2lo_done, n + 1)
                expert_hidden(n, range(0, 3), first)
                pe.wait_ge(t1_done, 4 * n + 4)
                split3(M[:], whi[:, 2 * C:], wlo[:, 2 * C:], x2hi[:], x2lo[:]).then_inc(route_ready, 1)
                expert_hidden(n, range(3, 6), first)
                wait_alone(pe, route_copied, n + 1)
                for s in range(SPB):
                    ins = nc.tensor.transpose(M[:, s * E:(s + 1) * E], gt_sb[:, s * TT:(s + 1) * TT], id_sb[0:E, 0:E])
                ins.then_inc(route_t_ready, 1)
                expert_hidden(n, range(6, NCH), first)

            pe.wait_ge(t_half, STEPS)
            tokens_first(0)
            pe.wait_ge(t0_done, 1)
            channels_first(0)
            project_q(0)
            project_k(0)
            project_v(0)
            body(0, first=True)
            with pe.Fori(1, NBLK - 1) as n:
                body(n)
            body(NBLK - 1, last=True)
            for s in range(SPB):
                expert_out(NBLK - 1, [(s, c) for c in range(NCH)])


def kernel(x, L0_conv_w_i2s, L0_conv_w_s2s, L0_conv_w_skip, L0_conv_b_skip, L1_attn_Wq, L1_attn_Wk, L1_attn_Wv,
           L1_attn_Wp, L1_attn_bp, L1_ffn_gate_w, L1_ffn_gate_b, L1_ffn_w1, L1_ffn_b1, L1_ffn_w2, L1_ffn_b2):
    import ml_dtypes
    import numpy as np
    import concourse.bacc as bacc
    from concourse.bass_utils import run_bass_kernel_spmd

    f = np.float32
    bf = ml_dtypes.bfloat16
    GROUP = 3
    a = {}
    xp = np.zeros((C, ROWS, B, PADW), f)
    xp[:, :, :, 1:] = np.asarray(x).transpose(1, 2, 0, 3)
    a["x"] = xp.reshape(C, -1)
    per = FEAT // GROUP
    w = np.asarray(L0_conv_w_i2s)[:, :, 0, 0:2].reshape(GROUP, 4, per, C, 2).transpose(3, 4, 1, 0, 2)
    w = w.reshape(C, 2, 4, FEAT)
    wi = np.zeros((C, 2, 2, GATE_M), f)
    ws_a = np.zeros((GATE_M, 2, GATE_M), f)
    ws_b = np.zeros((GATE_M, 2, GATE_M), f)
    s2s = np.asarray(L0_conv_w_s2s)[:, :, 0, :].reshape(4, FEAT, FEAT, 3).transpose(2, 3, 0, 1)
    group = np.arange(C) * GROUP // C
    seen = (np.repeat(np.arange(GROUP), per)[None, :] >= group[:, None]).astype(f)
    wi_mask = np.zeros((C, 2, GATE_M), f)
    for g in range(4):
        c, o = g // 2, 64 * (g % 2)
        wi[:, :, c, o:o + FEAT] = w[:, :, g]
        wi_mask[:, c, o:o + FEAT] = seen
        ws_a[0:FEAT, c, o:o + FEAT] = s2s[:, 0, g]
        ws_a[64:, c, o:o + FEAT] = s2s[:, 1, g]
        ws_b[0:FEAT, c, o:o + FEAT] = s2s[:, 2, g]
    a["wi"], a["wi_mask"], a["ws_a"], a["ws_b"] = wi, wi_mask, ws_a, ws_b
    a["wk_skip"] = np.zeros((GATE_M, C), f)
    a["wk_skip"][0:FEAT] = np.asarray(L0_conv_w_skip)[:, :, 0, 0].T
    a["skip_mask"] = np.zeros((GATE_M, C), f)
    a["skip_mask"][0:FEAT] = group[None, :] >= (np.arange(FEAT) * GROUP // FEAT)[:, None]
    a["b_skip"] = np.asarray(L0_conv_b_skip).reshape(C, 1)
    a["wq"], a["wk"], a["wv"] = (np.asarray(z).transpose(1, 0, 2).reshape(C, C)
                                 for z in (L1_attn_Wq, L1_attn_Wk, L1_attn_Wv))
    wp = np.zeros((3, VW, 2, C), f)
    wp[:, 0:HS] = np.asarray(L1_attn_Wp).reshape(2, 3, HS, C).transpose(1, 2, 0, 3)
    a["wp"] = wp.reshape(3 * VW, 2, C)
    a["bp"] = np.broadcast_to(np.asarray(L1_attn_bp), (128, C))
    gw = np.zeros((C, 128), f)
    gw[:, 0:E] = np.asarray(L1_ffn_gate_w)
    a["gate_w"] = gw
    a["gate_b"] = np.broadcast_to(np.tile(np.asarray(L1_ffn_gate_b), SPB), (128, SPB * E))
    a["w1"] = np.asarray(L1_ffn_w1).transpose(1, 0, 2).reshape(C, E * HID)
    a["b1"] = np.asarray(L1_ffn_b1).reshape(NCH, 128).T
    a["w2"] = np.asarray(L1_ffn_w2).reshape(NCH, 128, C).transpose(1, 0, 2)
    a["b2"] = np.broadcast_to(np.asarray(L1_ffn_b2).reshape(1, E * C), (2, E * C))
    a["ident"] = np.eye(128, dtype=f)
    a["ident_bf"] = np.eye(128).astype(bf)
    t, k = np.arange(TT)[:, None], np.arange(TT)[None, :]
    masked = np.where(k <= t, 0.0, float(ml_dtypes.finfo(bf).min)).astype(bf)
    a["causal_bf"] = np.broadcast_to(masked[:, None, :], (128, HG[0], TT))
    e, j = np.arange(E)[:, None], np.arange(E)[None, :]
    a["lower"] = np.broadcast_to((j < e).astype(f).reshape(1, E * E), (128, E * E))

    nc = bacc.Bacc("TRN2", target_bir_lowering=False, num_devices=1)
    arrays, args = {}, {}
    for name, v in a.items():
        v = np.ascontiguousarray(v)
        arrays[f"in_{name}"] = v
        args[name] = nc.dram_tensor(f"in_{name}", v.shape, mybir.dt.from_np(v.dtype), kind="ExternalInput").ap()
    args["out"] = nc.dram_tensor("out_y", (NBLK, 128, SPB, C), F32, kind="ExternalOutput").ap()
    hybrid_kernel(nc, **args)
    r = run_bass_kernel_spmd(nc, [arrays], core_ids=[0])
    y = r.results[0]["out_y"].reshape(NBLK, ROWS // 2, W, 2, 2, C)
    return y.transpose(0, 3, 5, 4, 1, 2).reshape(B, C, ROWS, W)
```

```python
from contextlib import ExitStack

import concourse.bass as bass
from concourse import mybir

F32 = mybir.dt.float32
F32R = mybir.dt.float32r
BF16 = mybir.dt.bfloat16
ALU = mybir.AluOpType
ACT = mybir.ActivationFunctionType
AX = mybir.AxisListType

B, C, ROWS, W = 16, 96, 16, 16
FEAT = 48
PADW = W + 1
HPADW = W + 2
GATE_M = 64 + FEAT
HALF = B // 2
HC = HALF * W
HEADS, HS = 6, 16
VW = 32
VB = 3 * VW + HS
TT = 128
SPB = 4
BT = SPB * TT
NBLK = B * ROWS * W // BT
STEPS = 2 * ROWS
E, HID = 4, 384
NCH = E * HID // 128
CPE = HID // 128
SCALE = float(C) ** -0.5
GATE_STEPS = 14

HG = (3, 2)
UNITS = [(a, t, h) for a in range(2) for t in range(2) for h in range(0, HEADS, HG[t])]
NU = len(UNITS)
TILE_END = [1 + max(u for u, (a, t, _) in enumerate(UNITS) if 2 * a + t == s) for s in range(SPB)]
FILL = [16, 3, 3, 2, 3, 3, 2, 2, 2, 0]
TAIL = SPB * NCH - sum(FILL)
TAIL_EARLY = min(TAIL, 9)
PT_ON_ACT = (1, 2, 4, 6, 8, 9)
EARLY_T0, EARLY_XT = 1, 4


def hybrid_kernel(nc, x, w_input, w_state, b_skip, wq, wk, wv, wp, bp,
                  gate_w, gate_b, w1, b1, w2, b2, ident, ident_bf, causal_bf, lower, out):
    with ExitStack() as ctx:
        def sb(name, shape, dt=F32):
            return ctx.enter_context(nc.sbuf_tensor(name, shape, dt))

        def bank(name):
            return ctx.enter_context(nc.psum_tensor(name, [128, 512], F32))

        def sem(name):
            return ctx.enter_context(nc.semaphore(name))

        id_sb = sb("id_sb", [128, 128])
        idb_sb = sb("idb_sb", [128, 128], BF16)
        causal_sb = sb("causal_sb", [128, HG[0], 128], BF16)
        lower_sb = sb("lower_sb", [128, E * E])
        win_sb = sb("win_sb", [C, 6, GATE_M])
        wi_sb = win_sb[:, 0:4].rearrange("p (t c) m -> p t c m", t=2)
        wim_sb = win_sb[:, 4:6]
        wst_sb = sb("wst_sb", [GATE_M, 4 * GATE_M + 2 * C])
        wsa_sb = wst_sb[:, 0:2 * GATE_M].rearrange("p (c m) -> p c m", c=2)
        wsb_sb = wst_sb[:, 2 * GATE_M:4 * GATE_M].rearrange("p (c m) -> p c m", c=2)
        wsk_sb = wst_sb[:, 4 * GATE_M:4 * GATE_M + C]
        wskm_sb = wst_sb[:, 4 * GATE_M + C:]
        bsk_sb = sb("bsk_sb", [C, 1])
        wraw = sb("wraw", [C, 2 * C + 128])
        whi = sb("whi", [C, 2 * C + 128], F32R)
        wlo = sb("wlo", [C, 2 * C + 128], F32R)
        wv_sb = sb("wv_sb", [C, C])
        wp_sb = sb("wp_sb", [C, C])
        bp_sb = sb("bp_sb", [128, C])
        gb_sb = sb("gb_sb", [128, SPB * E])
        w1hi = sb("w1hi", [C, E * HID], F32R)
        w1lo = sb("w1lo", [C, E * HID], F32R)
        b1_sb = sb("b1_sb", [128, NCH])
        w2_sb = sb("w2_sb", [128, NCH, C])
        b2_sb = sb("b2_sb", [2, E * C])
        b2t = sb("b2t", [2, E * C], F32R)
        b2l = sb("b2l", [2, E * C])
        b2p = sb("b2p", [2, E * C])
        b2hl = sb("b2hl", [2, E * C], F32R)
        ones2 = sb("ones2", [2, 128], F32R)
        nhalf = sb("nhalf", [128, SPB])
        x_pad = sb("x_pad", [C, ROWS * B * PADW])
        h_pad = sb("h_pad", [GATE_M, B, HPADW])
        t_ig = sb("t_ig", [FEAT, 2, 2, HC])
        t_fg = sb("t_fg", [FEAT, 2, 2, HC])
        g1 = sb("g1", [FEAT, 2, HC])
        fc = sb("fc", [FEAT, 2, HC])
        ig = sb("ig", [FEAT, 2, HC])
        c4 = sb("c4", [FEAT, 2, HC])
        c2 = sb("c2", [FEAT, 2, HC])
        tc_sb = sb("tc_sb", [FEAT, 2, HC])
        t_cm = sb("t_cm", [C, NBLK * BT])
        t_st = sb("t_st", [C, BT])
        t0 = sb("t0", [128, SPB, C])
        tb = sb("tb", [128, SPB, C])
        st1 = sb("st1", [128, SPB, 6])
        mv1 = sb("mv1", [128, SPB, 2])
        ve1 = sb("ve1", [128, SPB])
        rs1 = sb("rs1", [128, SPB])
        xh = sb("xh", [128, SPB, C])
        x1hi = sb("x1hi", [C, BT], F32R)
        x1lo = sb("x1lo", [C, BT], F32R)
        x1f = sb("x1f", [C, BT])
        q_cur = sb("q_cur", [C, 2, BT], F32R)
        q_st = sb("q_st", [C, 2, BT], F32R)
        k_cur = sb("k_cur", [C, 2, BT], F32R)
        k_bd = sb("k_bd", [C, 2, 2, 2, 3, 2 * TT], F32R)
        v_cur = sb("v_cur", [128, SPB, 2, VB])
        nmax = sb("nmax", [128, 3, HG[0]])
        den = sb("den", [128, 3, HG[0]])
        rden = sb("rden", [128, 3, HG[0]])
        p_sb = sb("p_sb", [128, 3, 512])
        pt_sb = sb("pt_sb", [128, 2, 512])
        o_t = sb("o_t", [C, TT])
        t1 = sb("t1", [128, SPB, C])
        t1p = sb("t1p", [128, SPB, C])
        st2 = sb("st2", [128, SPB, 6])
        mv2 = sb("mv2", [128, SPB, 2])
        ve2 = sb("ve2", [128, SPB])
        rs2 = sb("rs2", [128, SPB])
        xh2 = sb("xh2", [128, SPB, C])
        x2hi = sb("x2hi", [C, BT], F32R)
        x2lo = sb("x2lo", [C, BT], F32R)
        gt_sb = sb("gt_sb", [E, BT])
        gl = sb("gl", [128, SPB, E])
        gm = sb("gm", [128, SPB])
        gd = sb("gd", [128, SPB, E])
        ge = sb("ge", [128, SPB, E])
        gtr = sb("gtr", [128, SPB, E, E])
        geq = sb("geq", [128, SPB, E, E])
        geo = sb("geo", [128, SPB, E, E])
        gbt = sb("gbt", [128, SPB, E, E])
        grk = sb("grk", [128, SPB, E])
        gkp = sb("gkp", [128, SPB, E])
        gs = sb("gs", [128, SPB])
        gs2 = sb("gs2", [128, SPB])
        gdn = sb("gdn", [128, SPB])
        grd = sb("grd", [128, SPB])
        gw = sb("gw", [128, SPB, E])
        hid = sb("hid", [128, NCH, BT])
        w1raw = hid[0:C, 0:3, :].rearrange("p a b -> p (a b)")
        y_sb = sb("y_sb", [128, SPB, C])

        M = bank("M")
        A = bank("A")
        S = [bank("S0"), bank("S1")]
        T = bank("T")
        F = [bank("F0"), bank("F1"), bank("F2")]
        G = F + [A]
        L1 = [F[0], A, F[1], F[2]]
        L2 = [F[0], F[2], F[1], F[2]]
        K = [M, T]

        def last_chunk(bank):
            return max(c for c in range(NCH) if L1[c % 4] is bank)

        gates_ready = sem("gates_ready")
        skip_ready = sem("skip_ready")
        tt_ready = sem("tt_ready")
        xt_ready = sem("xt_ready")
        q_ready = sem("q_ready")
        k_ready = sem("k_ready")
        v_ready = sem("v_ready")
        scores_ready = sem("scores_ready")
        pt_ready = sem("pt_ready")
        av_ready = sem("av_ready")
        proj_ready = sem("proj_ready")
        x2t_ready = sem("x2t_ready")
        route_ready = sem("route_ready")
        route_t_ready = sem("route_t_ready")
        hid_ready = sem("hid_ready")
        y_ready = sem("y_ready")
        gates_tanh = sem("gates_tanh")
        cell_tanh = sem("cell_tanh")
        t0_done = sem("t0_done")
        x1hi_done = sem("x1hi_done")
        qhi_done = sem("qhi_done")
        khi_done = sem("khi_done")
        v_done = sem("v_done")
        exp_done = sem("exp_done")
        ot_done = sem("ot_done")
        x2hi_done = sem("x2hi_done")
        route_copied = sem("route_copied")
        route_exp = sem("route_exp")
        gelu_done = sem("gelu_done")
        cell_dve = sem("cell_dve")
        h_ready = sem("h_ready")
        t_half = sem("t_half")
        ln1_stats = sem("ln1_stats")
        ln1_aggr = sem("ln1_aggr")
        xh_done = sem("xh_done")
        x1lo_done = sem("x1lo_done")
        qlo_done = sem("qlo_done")
        klo_done = sem("klo_done")
        max_done = sem("max_done")
        rden_done = sem("rden_done")
        pt_done = sem("pt_done")
        t1_done = sem("t1_done")
        ln2_stats = sem("ln2_stats")
        ln2_aggr = sem("ln2_aggr")
        xh2_done = sem("xh2_done")
        x2lo_done = sem("x2lo_done")
        route_dve = sem("route_dve")
        comb = sem("comb")
        scaled = sem("scaled")
        rs1_step = sem("rs1_step")
        rs2_step = sem("rs2_step")
        tb_done = sem("tb_done")
        x1f_done = sem("x1f_done")
        t1p_done = sem("t1p_done")
        w_input_in = sem("w_input_in")
        w_rec_in = sem("w_rec_in")
        x_in = [sem(f"x_in{i}") for i in range(4)]
        w_in = sem("w_in")
        w1_in = sem("w1_in")
        t_staged = sem("t_staged")
        q_in = [sem("q_in0"), sem("q_in1")]
        q_in_first = [sem("q_in_first0"), sem("q_in_first1")]
        kbd_in = [[sem(f"kbd_in{a}{g}") for g in range(2)] for a in range(2)]
        y_out = sem("y_out")
        zeroed = sem("zeroed")
        w_dve = sem("w_dve")
        w_act = sem("w_act")

        W_REC, W_QK, W_ALL = 4, 5, 10
        N_WIN = 14
        block = ctx.enter_context(nc.Block())

        def x_row(r0):
            return x_pad[:, bass.ds(r0 * (B * PADW), B * PADW)].rearrange("p (b w) -> p b w", w=PADW)

        KBD = 6 * 16
        TRI = 3 * HS

        def out_parts(slot):
            return [divmod(i, NCH) for i in range(sum(FILL[:slot]), sum(FILL[:slot + 1]))]

        def wait_alone(eng, semaphore, value):
            if not isinstance(value, int):
                value = eng.snap(eng.to_reg(value))
            eng.wait_ge(zeroed, 5)
            eng.wait_ge(semaphore, value)

        def as_f32(ap):
            return ap.bitcast(F32)

        def queries_taken(eng, n, g):
            if isinstance(n, int) and n == 0:
                eng.wait_ge(q_in_first[g], 32)
            else:
                eng.wait_ge(q_in[g], 32 * n)

        def load_queries(eng, g, taken):
            for part in range(2):
                eng.dma_start(as_f32(q_st[part * TRI:(part + 1) * TRI, g, :]),
                              as_f32(q_cur[g * TRI:(g + 1) * TRI, part, :])).then_inc(taken[g], 16)

        @block.sync
        def _(sp):
            row = B * PADW
            sp.dma_start(win_sb[:], w_input).then_inc(w_input_in, 16)
            for i, (r0, r1) in enumerate(((0, 2), (2, 4), (4, 10), (10, ROWS))):
                sp.dma_start(x_pad[:, r0 * row:r1 * row], x[:, r0 * row:r1 * row]).then_inc(x_in[i], 16)
                if i == 0:
                    sp.dma_start(wst_sb[:], w_state).then_inc(w_rec_in, 16)
                if i == 1:
                    sp.dma_start(bsk_sb[:], b_skip).then_inc(w_rec_in, 16)
                if i == 3:
                    for dst, src in ((id_sb[:], ident), (idb_sb[:], ident_bf), (causal_sb[:], causal_bf),
                                     (lower_sb[:], lower), (wraw[:, 0:C], wq), (wraw[:, C:2 * C], wk),
                                     (wraw[:, 2 * C:], gate_w), (wv_sb[:], wv), (wp_sb[:], wp), (bp_sb[:], bp),
                                     (gb_sb[:], gate_b), (b1_sb[:], b1), (b2_sb[:], b2), (w2_sb[:], w2)):
                        sp.dma_start(dst, src).then_inc(w_in, 16)
                    sp.dma_start(w1raw, w1).then_inc(w1_in, 16)

            def stage(n):
                sp.dma_start(t_st[:], t_cm[:, bass.ds(n * BT, BT)]).then_inc(t_staged, 16)

            def load_keys(a, g):
                cols = slice(a * 2 * TT, (a + 1) * 2 * TT)
                for i in range(3):
                    h = 3 * g + i
                    rows_h = slice(h * HS, (h + 1) * HS)
                    upper, lower_ = slice(i * HS, (i + 1) * HS), slice(TRI + i * HS, TRI + (i + 1) * HS)
                    sp.dma_start(as_f32(k_bd[upper, a, :, g, i, :]), as_f32(k_cur[rows_h, :, cols])
                                 ).then_inc(kbd_in[a][g], 16)
                    sp.dma_start(as_f32(k_bd[lower_, a, 0, g, i, :]), as_f32(k_cur[rows_h, 0, cols])
                                 ).then_inc(kbd_in[a][g], 16)

            def store_y(n):
                wait_alone(sp, comb, 16 * n + 16)
                sp.dma_start(out[bass.ds(n, 1)].rearrange("a p s c -> p (a s) c"), y_sb[:]).then_inc(y_out, 16)

            def body(n, first=False, store=True, more=True):
                if first:
                    sp.wait_ge(klo_done, 1)
                    load_keys(0, 0)
                    load_keys(0, 1)
                else:
                    wait_alone(sp, scores_ready, NU * n)
                    wait_alone(sp, qlo_done, n + 1)
                    load_queries(sp, 0, q_in)
                    load_queries(sp, 1, q_in)
                    wait_alone(sp, klo_done, n + 1)
                    load_keys(0, 0)
                    load_keys(0, 1)
                if store:
                    store_y(n - 2)
                load_keys(1, 0)
                load_keys(1, 1)
                if more:
                    wait_alone(sp, tt_ready, n + 2)
                    stage(n + 2)

            sp.wait_ge(zeroed, 5)
            sp.wait_ge(t_half, STEPS)
            stage(1)
            body(0, first=True, store=False)
            body(1, store=False)
            with sp.Fori(2, NBLK - 2) as n:
                body(n)
            for n in range(NBLK - 2, NBLK):
                body(n, more=False)
            store_y(NBLK - 2)
            for s0, s1 in ((0, SPB - 1), (SPB - 1, SPB)):
                sp.wait_ge(comb, 16 * (NBLK - 1) + 4 * s1)
                sp.dma_start(out[NBLK - 1, :, s0:s1], y_sb[:, s0:s1]).then_inc(y_out, 16)
            sp.wait_ge(y_out, 16 * (NBLK + 1))

        @block.gpsimd
        def _(pool):
            nc.gpsimd.memset(h_pad[:], 0.0).then_inc(zeroed, 1)
            nc.gpsimd.memset(c2[:], 0.0).then_inc(zeroed, 1)
            nc.gpsimd.memset(as_f32(k_bd[:]), 0.0).then_inc(zeroed, 1)
            nc.gpsimd.memset(v_cur[:], 0.0).then_inc(zeroed, 1)
            nc.gpsimd.memset(nhalf[:], -0.5).then_inc(zeroed, 1)
            pool.wait_ge(zeroed, 5)

            def rstd1(n):
                wait_alone(pool, ln1_aggr, 4 * n + 4)
                nc.gpsimd.tensor_scalar(ve1[:], mv1[:, :, 1], 1e-5, None, ALU.add).then_inc(rs1_step, 1)
                pool.wait_ge(rs1_step, 2 * n + 1)
                nc.gpsimd.tensor_tensor(rs1[:], ve1[:], nhalf[:], ALU.pow).then_inc(rs1_step, 1)

            def rstd2(n, s):
                wait_alone(pool, ln2_aggr, 4 * n + s + 1)
                nc.gpsimd.tensor_scalar(ve2[:, s:s + 1], mv2[:, s, 1:2], 1e-5, None, ALU.add).then_inc(rs2_step, 1)
                pool.wait_ge(rs2_step, 8 * n + 2 * s + 1)
                nc.gpsimd.tensor_tensor(rs2[:, s:s + 1], ve2[:, s:s + 1], nhalf[:, 0:1], ALU.pow).then_inc(rs2_step, 1)

            def residual(n):
                pool.wait_ge(t0_done, n + 1)
                nc.gpsimd.tensor_tensor(tb[:], t0[:], bp_sb[:].unsqueeze(1).to_broadcast((128, SPB, C)),
                                        ALU.add).then_inc(tb_done, 1)

            def scale(n, u):
                wait_alone(pool, rden_done, NU * n + u + 1)
                _, t, _ = UNITS[u]
                nk = TT * (t + 1)
                for i in range(HG[t]):
                    p = p_sb[:, u % 3, i * nk:(i + 1) * nk]
                    last = nc.gpsimd.tensor_scalar(p, p, rden[:, u % 3, i:i + 1], 1.0, ALU.mult, ALU.mult)
                last.then_inc(scaled, 1)

            def x1_whole(n):
                wait_alone(pool, x1lo_done, n + 1)
                nc.gpsimd.tensor_tensor(x1f[:], as_f32(x1hi[:]), as_f32(x1lo[:]), ALU.add).then_inc(x1f_done, 1)

            def keep_t1(n, first):
                wait_alone(pool, t1_done, 4 * n + 4)
                if not first:
                    wait_alone(pool, comb, 16 * n)
                nc.gpsimd.tensor_copy(t1p[:], t1[:]).then_inc(t1p_done, 1)

            def body(n, first=False, last=False):
                scale(n, 0)
                for j in range(NU):
                    if j + 1 < NU:
                        scale(n, j + 1)
                    if j == EARLY_T0 + 1 and not last:
                        rstd1(n + 1)
                    for s in range(SPB - 1):
                        if j == TILE_END[s] + 1:
                            rstd2(n, s)
                rstd2(n, SPB - 1)
                keep_t1(n, first)
                if not last:
                    residual(n + 1)
                    x1_whole(n + 1)

            pool.wait_ge(w_in, 16 * N_WIN)
            rstd1(0)
            residual(0)
            x1_whole(0)
            pool.wait_ge(qlo_done, 1)
            load_queries(nc.gpsimd, 0, q_in_first)
            load_queries(nc.gpsimd, 1, q_in_first)
            body(0, first=True)
            with pool.Fori(1, NBLK - 1) as n:
                body(n)
            body(NBLK - 1, last=True)

        def take_pt(eng, n, u, first=False):
            t = UNITS[u][1]
            w = HG[t] * (t + 1) * TT
            eng.wait_ge(pt_ready, NU * n + u + 1)
            if u >= 2 or not first:
                eng.wait_ge(av_ready, NU * n + u - 1)
            copy = nc.scalar.copy if u in PT_ON_ACT else nc.vector.tensor_copy
            copy(pt_sb[:, u % 2, 0:w], T[:, 0:w]).then_inc(pt_done, 1)

        @block.scalar
        def _(act):
            def cell_gates(m, hb, src):
                act.wait_ge(gates_ready, m + 1)
                v = src[:, 0:2 * HC].rearrange("p (c n) -> p c n", c=2)
                nc.scalar.activation(t_fg[:, hb], v[64:64 + FEAT], ACT.Tanh, scale=0.5).then_inc(gates_tanh, 1)
                nc.scalar.activation(t_ig[:, hb], v[0:FEAT], ACT.Tanh, scale=0.5).then_inc(gates_tanh, 1)

            def cell_out(m, hb):
                act.wait_ge(cell_dve, 5 * m + 4)
                nc.scalar.activation(tc_sb[:, hb], c4[:, hb], ACT.Tanh, scale=0.25).then_inc(cell_tanh, 1)

            def rec0(it):
                for q in range(4):
                    m = 4 * it + q
                    cell_gates(m, q % 2, G[q])
                    cell_out(m, q % 2)

            rec0(0)
            with act.Fori(1, ROWS // 2) as it:
                rec0(it)
            act.wait_ge(w_in, 16 * N_WIN)
            nc.scalar.copy(whi[:], wraw[:]).then_inc(w_act, 1)

            def take_t0(n, first=False):
                act.wait_ge(tt_ready, n + 1)
                if not first:
                    act.wait_ge(tb_done, n)
                nc.scalar.copy(t0[:], M[:, 0:SPB * C].rearrange("p (s c) -> p s c", s=SPB)).then_inc(t0_done, 1)

            def take_x1(n):
                act.wait_ge(xt_ready, n + 1)
                nc.scalar.copy(x1hi[:], M[0:C, :]).then_inc(x1hi_done, 1)

            def take_q(n):
                act.wait_ge(q_ready, n + 1)
                nc.scalar.mul(q_cur[:, 0, :], S[0][0:C, :], SCALE).then_inc(qhi_done, 1)

            def take_k(n):
                act.wait_ge(k_ready, n + 1)
                nc.scalar.copy(k_cur[:, 0, :], S[1][0:C, :]).then_inc(khi_done, 1)

            def take_v(n):
                act.wait_ge(v_ready, n + 1)
                nc.scalar.copy(v_cur[:, :, :, 0:3 * VW].rearrange("p s b (u w) -> p s b u w", w=VW)[..., 0:HS],
                               M[:, 0:SPB * C].rearrange("p (s b u d) -> p s b u d", s=SPB, b=2, u=3)
                               ).then_inc(v_done, 1)

            def exps(n, u, first=False):
                act.wait_ge(max_done, NU * n + u + 1)
                if u >= 3 or not first:
                    act.wait_ge(pt_ready, NU * n + u - 2)
                _, t, _ = UNITS[u]
                nk = TT * (t + 1)
                for i in range(HG[t]):
                    last = nc.scalar.activation(p_sb[:, u % 3, i * nk:(i + 1) * nk], S[u % 2][:, i * nk:(i + 1) * nk],
                                                ACT.Exp, bias=nmax[:, u % 3, i:i + 1],
                                                accum_out=den[:, u % 3, i:i + 1])
                last.then_inc(exp_done, 1)

            def heads_out(n, s, first=False):
                act.wait_ge(av_ready, NU * n + TILE_END[s])
                if s or not first:
                    act.wait_ge(proj_ready, 4 * n + s)
                nc.scalar.copy(o_t[:], A[0:C, 0:TT]).then_inc(ot_done, 1)

            def body(n, first=False, last=False):
                if not first:
                    act.wait_ge(route_dve, GATE_STEPS * (n - 1) + 3)
                    nc.scalar.activation(ge[:], gd[:], ACT.Exp).then_inc(route_exp, 1)
                exps(n, 0, first)
                take_v(n)
                exps(n, 1, first)
                for j in range(NU):
                    for s in range(SPB - 1):
                        if j == TILE_END[s]:
                            heads_out(n, s, first)
                    if j in PT_ON_ACT:
                        take_pt(act, n, j, first)
                    if j + 2 < NU:
                        exps(n, j + 2, first)
                    if j == EARLY_T0 and not last:
                        take_t0(n + 1)
                    if j == EARLY_XT and not last:
                        take_x1(n + 1)
                heads_out(n, SPB - 1, first)
                if not last:
                    for per_sample in kbd_in:
                        for taken in per_sample:
                            act.wait_ge(taken, KBD * (n + 1))
                    for g in range(2):
                        queries_taken(act, n, g)
                    take_q(n + 1)
                    take_k(n + 1)
                act.wait_ge(x2t_ready, n + 1)
                nc.scalar.copy(x2hi[:], T[0:C, :]).then_inc(x2hi_done, 1)
                if not first:
                    act.wait_ge(y_ready, 4 * n)
                for c in range(NCH):
                    act.wait_ge(hid_ready, NCH * n + c + 1)
                    nc.scalar.activation(hid[:, c, :], L1[c % 4][:], ACT.Gelu, bias=b1_sb[:, c:c + 1]
                                         ).then_inc(gelu_done, 1)
                    if c == 3:
                        act.wait_ge(route_ready, n + 1)
                        nc.scalar.copy(gt_sb[:], M[0:E, :]).then_inc(route_copied, 1)

            take_t0(0, first=True)
            take_x1(0)
            take_k(0)
            take_q(0)
            nc.scalar.copy(b2t[:], b2_sb[:]).then_inc(w_act, 1)
            act.wait_ge(w1_in, 16)
            nc.scalar.copy(w1hi[:], w1raw).then_inc(w_act, 1)
            body(0, first=True)
            with act.Fori(1, NBLK - 1) as n:
                body(n)
            body(NBLK - 1, last=True)
            act.wait_ge(route_dve, GATE_STEPS * (NBLK - 1) + 3)
            nc.scalar.activation(ge[:], gd[:], ACT.Exp).then_inc(route_exp, 1)

        @block.vector
        def _(dve):
            V = nc.vector
            steps = [0]

            def setup_step(ins):
                steps[0] += 1
                ins.then_inc(w_dve, 1)

            dve.wait_ge(w_input_in, 16)
            setup_step(V.tensor_tensor(wi_sb[:, 1], wi_sb[:, 1], wim_sb[:], ALU.mult))
            dve.wait_ge(w_rec_in, 16 * 2)
            setup_step(V.tensor_scalar(wsa_sb[:], wsa_sb[:], 0.5, None, ALU.mult))
            setup_step(V.tensor_scalar(wsb_sb[:], wsb_sb[:], 0.5, None, ALU.mult))
            setup_step(V.scalar_tensor_tensor(wsk_sb[:], wsk_sb[:], 0.5, wskm_sb[:], ALU.mult, ALU.mult))
            dve.wait_ge(zeroed, 2)

            def split_qk_weights():
                dve.wait_ge(w_act, 1)
                setup_step(V.tensor_tensor(wlo[:], wraw[:], as_f32(whi[:]), ALU.subtract))

            def split_expert_weights():
                setup_step(V.memset(as_f32(ones2[:]), 1.0))
                dve.wait_ge(w_act, 2)
                setup_step(V.tensor_tensor(b2l[:], b2_sb[:], as_f32(b2t[:]), ALU.subtract))
                setup_step(V.tensor_scalar(b2p[:], as_f32(b2t[:]), id_sb[0:2, 0:1], None, ALU.mult))
                dve.wait_ge(w_act, 3)
                setup_step(V.tensor_tensor(w1lo[:], w1raw, as_f32(w1hi[:]), ALU.subtract))
                dve.wait_ge(w_dve, W_ALL - 1)
                setup_step(V.scalar_tensor_tensor(b2hl[:], b2l[:], id_sb[0:2, 1:2], b2p[:], ALU.mult, ALU.add))
                assert steps[0] == W_ALL

            def cell(m, hb):
                dve.wait_ge(gates_tanh, 2 * m + 1)
                V.tensor_scalar(g1[:, hb], t_fg[:, hb, 1], 1.0, None, ALU.add).then_inc(cell_dve, 1)
                V.scalar_tensor_tensor(fc[:, hb], t_fg[:, hb, 0], 1.0, c2[:, hb], ALU.add, ALU.mult).then_inc(cell_dve, 1)
                dve.wait_ge(gates_tanh, 2 * m + 2)
                dve.wait_ge(cell_dve, 5 * m + 1)
                V.scalar_tensor_tensor(ig[:, hb], t_ig[:, hb, 1], 1.0, g1[:, hb], ALU.add, ALU.mult).then_inc(cell_dve, 1)
                dve.wait_ge(cell_dve, 5 * m + 3)
                V.tensor_tensor(c4[:, hb], fc[:, hb], ig[:, hb], ALU.add).then_inc(cell_dve, 1)
                dve.wait_ge(cell_dve, 5 * m + 4)
                V.tensor_scalar(c2[:, hb], c4[:, hb], 0.5, None, ALU.mult).then_inc(cell_dve, 1)

            def cell_h(m, hb, first=False):
                dve.wait_ge(cell_tanh, m + 1)
                if not first:
                    dve.wait_ge(skip_ready, m - 1)
                o = t_ig[:, hb, 0].rearrange("p (b w) -> p b w", w=W)
                t = tc_sb[:, hb].rearrange("p (b w) -> p b w", w=W)
                bs = slice(hb * HALF, (hb + 1) * HALF)
                V.scalar_tensor_tensor(h_pad[0:FEAT, bs, 1:1 + W], o, 1.0, t, ALU.add, ALU.mult).then_inc(h_ready, 1)
                V.scalar_tensor_tensor(h_pad[64:64 + FEAT, bs, 0:W], o, 1.0, t, ALU.add, ALU.mult).then_inc(h_ready, 1)

            def add_skip(m, hb, row):
                dve.wait_ge(skip_ready, m + 1)
                bs = slice(hb * HALF, (hb + 1) * HALF)
                dst = t_cm[:].rearrange("p (b t) -> p b t", t=ROWS * W)[:, bs, bass.ds(row * W, W)]
                V.scalar_tensor_tensor(dst, K[hb][0:C, 0:HC].rearrange("p (b w) -> p b w", w=W),
                                       bsk_sb[:, 0:1], x_row(row)[:, bs, 1:], ALU.add, ALU.add).then_inc(t_half, 1)

            def rec0(it, first):
                for q in range(4):
                    m, hb = 4 * it + q, q % 2
                    cell(m, hb)
                    cell_h(m, hb, first=first and q < 2)
                    if q >= 2 or not first:
                        add_skip(m - 2, hb, 2 * it + q // 2 - 1)

            dve.wait_ge(x_in[0], 16)
            rec0(0, True)
            for i in (1, 2, 3):
                dve.wait_ge(x_in[i], 16)
            with dve.Fori(1, ROWS // 2) as it:
                rec0(it, False)
            for hb in range(2):
                add_skip(STEPS - 2 + hb, hb, ROWS - 1)
            split_qk_weights()

            def norm1(n):
                dve.wait_ge(t0_done, n + 1)
                for s in range(SPB):
                    V.bn_stats(st1[:, s], t0[:, s]).then_inc(ln1_stats, 1)
                wait_alone(dve, ln1_stats, 4 * n + 4)
                for s in range(SPB):
                    V.bn_aggr(mv1[:, s], st1[:, s]).then_inc(ln1_aggr, 1)

            def normalize1(n):
                dve.wait_ge(rs1_step, 2 * n + 2)
                for s in range(SPB):
                    V.tensor_scalar(xh[:, s], t0[:, s], mv1[:, s, 0:1], rs1[:, s:s + 1],
                                    ALU.subtract, ALU.mult).then_inc(xh_done, 1)

            def x1_rest(n):
                dve.wait_ge(x1hi_done, n + 1)
                V.tensor_tensor(x1lo[:], M[0:C, :], as_f32(x1hi[:]), ALU.subtract).then_inc(x1lo_done, 1)

            def q_rest(n):
                dve.wait_ge(qhi_done, n + 1)
                V.scalar_tensor_tensor(q_cur[:, 1, :], S[0][0:C, :], SCALE, as_f32(q_cur[:, 0, :]), ALU.mult, ALU.subtract
                                       ).then_inc(qlo_done, 1)

            def k_rest(n):
                dve.wait_ge(khi_done, n + 1)
                V.tensor_tensor(k_cur[:, 1, :], S[1][0:C, :], as_f32(k_cur[:, 0, :]), ALU.subtract
                                ).then_inc(klo_done, 1)

            def row_max(n, u):
                _, t, _ = UNITS[u]
                nk = TT * (t + 1)
                dve.wait_ge(scores_ready, NU * n + u + 1)
                V.tensor_reduce(nmax[:, u % 3, 0:HG[t]], S[u % 2][:, 0:HG[t] * nk].rearrange("p (h k) -> p h k", k=nk),
                                AX.X, ALU.max, negate=True).then_inc(max_done, 1)

            def recip(n, u):
                dve.wait_ge(exp_done, NU * n + u + 1)
                hg = HG[UNITS[u][1]]
                V.reciprocal(rden[:, u % 3, 0:hg], den[:, u % 3, 0:hg]).then_inc(rden_done, 1)

            def attn_residual(n, s, first=False):
                dve.wait_ge(proj_ready, 4 * n + s + 1)
                dve.wait_ge(tb_done, n + 1)
                if s == 0 and not first:
                    dve.wait_ge(t1p_done, n)
                V.tensor_tensor(t1[:, s], M[:, 0:C], tb[:, s], ALU.add).then_inc(t1_done, 1)
                dve.wait_ge(t1_done, 4 * n + s + 1)
                V.bn_stats(st2[:, s], t1[:, s]).then_inc(ln2_stats, 1)
                wait_alone(dve, ln2_stats, 4 * n + s + 1)
                V.bn_aggr(mv2[:, s], st2[:, s]).then_inc(ln2_aggr, 1)

            def normalize2(n, s):
                dve.wait_ge(rs2_step, 8 * n + 2 * s + 2)
                V.tensor_scalar(xh2[:, s], t1[:, s], mv2[:, s, 0:1], rs2[:, s:s + 1],
                                ALU.subtract, ALU.mult).then_inc(xh2_done, 1)

            def route(n, part):
                base = GATE_STEPS * n
                ej = (128, SPB, E, E)
                of_j = ge[:].unsqueeze(2).to_broadcast(ej)
                of_e = ge[:].unsqueeze(3).to_broadcast(ej)
                if part == 0:
                    dve.wait_ge(route_t_ready, n + 1)
                    V.tensor_tensor(gl[:].rearrange("p s e -> p (s e)"), M[:, 0:SPB * E], gb_sb[:], ALU.add
                                    ).then_inc(route_dve, 1)
                    dve.wait_ge(route_dve, base + 1)
                    V.tensor_reduce(gm[:], gl[:], AX.X, ALU.max).then_inc(route_dve, 1)
                    dve.wait_ge(route_dve, base + 2)
                    V.tensor_tensor(gd[:], gl[:], gm[:].unsqueeze(2).to_broadcast((128, SPB, E)), ALU.subtract
                                    ).then_inc(route_dve, 1)
                    return
                if part == 2:
                    dve.wait_ge(route_dve, base + 9)
                    V.tensor_reduce(gs2[:], gkp[:], AX.X, ALU.add).then_inc(route_dve, 1)
                    V.tensor_reduce(gs[:], ge[:], AX.X, ALU.add).then_inc(route_dve, 1)
                    dve.wait_ge(route_dve, base + 11)
                    V.scalar_tensor_tensor(gdn[:], gs[:], 1e-9, gs2[:], ALU.mult, ALU.add).then_inc(route_dve, 1)
                    dve.wait_ge(route_dve, base + 12)
                    V.reciprocal(grd[:], gdn[:]).then_inc(route_dve, 1)
                    dve.wait_ge(route_dve, base + 13)
                    V.tensor_tensor(gw[:], gkp[:], grd[:].unsqueeze(2).to_broadcast((128, SPB, E)), ALU.mult
                                    ).then_inc(route_dve, 1)
                    dve.wait_ge(route_dve, base + 14)
                    return
                dve.wait_ge(route_exp, n + 1)
                V.tensor_tensor(gtr[:], of_j, of_e, ALU.is_gt).then_inc(route_dve, 1)
                V.tensor_tensor(geq[:], of_j, of_e, ALU.is_equal).then_inc(route_dve, 1)
                dve.wait_ge(route_dve, base + 5)
                V.tensor_tensor(geo[:].rearrange("p s e j -> p s (e j)"), geq[:].rearrange("p s e j -> p s (e j)"),
                                lower_sb[:].unsqueeze(1).to_broadcast((128, SPB, E * E)), ALU.mult).then_inc(route_dve, 1)
                dve.wait_ge(route_dve, base + 6)
                V.tensor_tensor(gbt[:], gtr[:], geo[:], ALU.add).then_inc(route_dve, 1)
                dve.wait_ge(route_dve, base + 7)
                V.tensor_reduce(grk[:], gbt[:], AX.X, ALU.add).then_inc(route_dve, 1)
                dve.wait_ge(route_dve, base + 8)
                V.scalar_tensor_tensor(gkp[:], grk[:], 1.5, ge[:], ALU.is_lt, ALU.mult).then_inc(route_dve, 1)

            def combine(n, s, first):
                dve.wait_ge(y_ready, 4 * n + s + 1)
                dve.wait_ge(t1p_done, n + 1)
                if s == 0 and not first:
                    dve.wait_ge(y_out, 16 * n)
                for e in range(E):
                    if e:
                        dve.wait_ge(comb, 16 * n + 4 * s + e)
                    V.scalar_tensor_tensor(y_sb[:, s], L2[s][:, e * C:(e + 1) * C], gw[:, s, e:e + 1],
                                           t1p[:, s] if e == 0 else y_sb[:, s], ALU.mult, ALU.add).then_inc(comb, 1)

            def body(n, first=False, second=False, last=False):
                if not first:
                    route(n - 1, 1)
                recip(n, 0)
                if first:
                    row_max(0, 1)
                else:
                    route(n - 1, 2)
                for j in range(NU):
                    if j + 2 < NU:
                        row_max(n, j + 2)
                    if j + 1 < NU:
                        recip(n, j + 1)
                    if j not in PT_ON_ACT:
                        take_pt(dve, n, j, first)
                    if j == EARLY_XT + 1 and not last:
                        x1_rest(n + 1)
                    if not first and j:
                        for s, c in out_parts(j - 1):
                            if c == NCH - 1:
                                combine(n - 1, s, second)
                    if not last:
                        if j == EARLY_T0 + 1:
                            norm1(n + 1)
                        if j == EARLY_T0 + 2:
                            normalize1(n + 1)
                    for s in range(SPB - 1):
                        if j == TILE_END[s] + 1:
                            attn_residual(n, s, first)
                        if j == TILE_END[s] + 2:
                            normalize2(n, s)
                attn_residual(n, SPB - 1)
                if not last:
                    q_rest(n + 1)
                normalize2(n, SPB - 1)
                if not last:
                    k_rest(n + 1)
                dve.wait_ge(x2hi_done, n + 1)
                V.tensor_tensor(x2lo[:], T[0:C, :], as_f32(x2hi[:]), ALU.subtract).then_inc(x2lo_done, 1)
                if not first:
                    for s in range(sum(FILL[:-1]) // NCH, SPB):
                        combine(n - 1, s, second)
                route(n, 0)
                if not last:
                    row_max(n + 1, 0)
                    row_max(n + 1, 1)

            norm1(0)
            normalize1(0)
            x1_rest(0)
            k_rest(0)
            q_rest(0)
            split_expert_weights()
            row_max(0, 0)
            body(0, first=True)
            body(1, second=True)
            with dve.Fori(2, NBLK - 1) as n:
                body(n)
            body(NBLK - 1, last=True)
            route(NBLK - 1, 1)
            route(NBLK - 1, 2)
            for s in range(SPB):
                combine(NBLK - 1, s, False)

        @block.tensor
        def _(pe):
            mm = nc.tensor.matmul

            def split3(dst, hi_l, lo_l, hi_r, lo_r, stop=True, **kw):
                mm(dst, hi_l, hi_r, start=True, stop=False, **kw)
                mm(dst, hi_l, lo_r, start=False, stop=False, **kw)
                return mm(dst, lo_l, hi_r, start=False, stop=stop, **kw)

            def input_part(m, q, row, ready=False, fresh=False):
                bs = slice(q % 2 * HALF, (q % 2 + 1) * HALF)
                if not fresh:
                    pe.wait_ge(gates_tanh, 2 * m - 6)
                xr = x_row(row)
                for c in range(2):
                    for tap in range(2):
                        last = mm(G[q][0:GATE_M, c * HC:(c + 1) * HC], wi_sb[:, tap, c], xr[:, bs, tap:tap + W],
                                  start=(c == 0 and tap == 0), stop=ready, skip_group_check=True)
                if ready:
                    last.then_inc(gates_ready, 1)

            def state_part(m, q):
                bs = slice(q % 2 * HALF, (q % 2 + 1) * HALF)
                pe.wait_ge(h_ready, 2 * m - 2)
                for c in range(2):
                    d = G[q][0:GATE_M, c * HC:(c + 1) * HC]
                    mm(d, wsa_sb[:, c], h_pad[:, bs, 0:W], start=False, stop=False, skip_group_check=True)
                    last = mm(d, wsb_sb[:, c], h_pad[:, bs, 2:2 + W], start=False, stop=True, skip_group_check=True)
                last.then_inc(gates_ready, 1)

            def skip(m, hb, fresh=False):
                bs = slice(hb * HALF, (hb + 1) * HALF)
                if not fresh:
                    pe.wait_ge(t_half, m - 1)
                mm(K[hb][0:C, 0:HC], wsk_sb[:], h_pad[:, bs, 1:1 + W], start=True, stop=True).then_inc(skip_ready, 1)

            def half_step(m, q, row, fresh=False, more=True):
                state_part(m, q)
                skip(m - 2, q % 2, fresh)
                if more:
                    input_part(m + 2, (q + 2) % 4, row + 1)

            pe.wait_ge(w_dve, 1)
            pe.wait_ge(x_in[0], 16)
            for m in range(4):
                input_part(m, m, m // 2, ready=m < 2, fresh=True)
            pe.wait_ge(w_dve, W_REC)
            pe.wait_ge(zeroed, 2)
            pe.wait_ge(x_in[1], 16)
            for m in (2, 3):
                half_step(m, m, m // 2, fresh=True)
            for i in (2, 3):
                pe.wait_ge(x_in[i], 16)
            with pe.Fori(1, ROWS // 2 - 1) as it:
                for q in range(4):
                    half_step(4 * it + q, q, 2 * it + q // 2)
            for m in range(STEPS - 4, STEPS):
                half_step(m, m % 4, m // 2, more=m < STEPS - 2)
            for hb in range(2):
                pe.wait_ge(h_ready, 2 * STEPS - 2 + 2 * hb)
                skip(STEPS - 2 + hb, hb)
            pe.wait_ge(w_in, 16 * N_WIN)

            def tokens_first(n):
                src = t_cm if isinstance(n, int) and n == 0 else t_st
                if src is t_st:
                    pe.wait_ge(t_staged, 16 * n)
                for s in range(SPB):
                    last = nc.tensor.transpose(M[:, s * C:(s + 1) * C], src[:, s * TT:(s + 1) * TT], id_sb[0:C, 0:C])
                last.then_inc(tt_ready, 1)

            def channels_first(n):
                pe.wait_ge(xh_done, 4 * n + 4)
                for s in range(SPB):
                    last = nc.tensor.transpose(M[0:C, s * TT:(s + 1) * TT], xh[:, s], id_sb[:])
                last.then_inc(xt_ready, 1)

            def project_q(n):
                pe.wait_ge(x1lo_done, n + 1)
                split3(S[0][0:C, :], whi[:, 0:C], wlo[:, 0:C], x1hi[:], x1lo[:]).then_inc(q_ready, 1)

            def project_k(n):
                split3(S[1][0:C, :], whi[:, C:2 * C], wlo[:, C:2 * C], x1hi[:], x1lo[:]).then_inc(k_ready, 1)

            def project_v(n):
                pe.wait_ge(x1f_done, n + 1)
                for s in range(SPB):
                    last = mm(M[:, s * C:(s + 1) * C], x1f[:, s * TT:(s + 1) * TT], wv_sb[:], start=True, stop=True)
                last.then_inc(v_ready, 1)

            def scores(n, u):
                a, t, h0 = UNITS[u]
                nh, nk, s = HG[t], TT * (t + 1), 2 * a + t
                if u >= 2:
                    pe.wait_ge(exp_done, NU * n + u - 1)
                elif u == 0:
                    pe.wait_ge(qlo_done, n + 1)
                    pe.wait_ge(klo_done, n + 1)
                if u < 2:
                    queries_taken(pe, n, u)
                if t == 0:
                    pe.wait_ge(kbd_in[a][h0 // 3], KBD * (n + 1))
                dst = S[u % 2][:, 0:nh * nk].rearrange("p (h k) -> p h k", k=nk)
                ts = slice(s * TT, (s + 1) * TT)
                for g in range(h0 // 3, (h0 + nh - 1) // 3 + 1):
                    i0, i1 = max(h0 - 3 * g, 0), min(h0 + nh - 3 * g, 3)
                    d = dst[:, 3 * g + i0 - h0:3 * g + i1 - h0]
                    mm(d, q_st[:, g, ts], k_bd[:, a, 0, g, i0:i1, 0:nk], start=(3 * g + i0 == h0), stop=False,
                       skip_group_check=True)
                    mm(d, q_st[:, g, ts], k_bd[:, a, 1, g, i0:i1, 0:nk], start=False, stop=False,
                       skip_group_check=True)
                mm(dst[:, :, nk - TT:nk], idb_sb[:], causal_sb[:, 0:nh, :], start=False, stop=True, skip_group_check=True
                   ).then_inc(scores_ready, 1)

            def probs_t(n, u, first=False):
                pe.wait_ge(scaled, NU * n + u + 1)
                if u:
                    pe.wait_ge(pt_done, NU * n + u)
                elif not first:
                    pe.wait_ge(x2lo_done, n)
                t = UNITS[u][1]
                for i in range(HG[t] * (t + 1)):
                    last = nc.tensor.transpose(T[:, i * TT:(i + 1) * TT], p_sb[:, u % 3, i * TT:(i + 1) * TT], id_sb[:])
                last.then_inc(pt_ready, 1)

            def values(n, u, first=False):
                a, t, h0 = UNITS[u]
                s = 2 * a + t
                pe.wait_ge(pt_done, NU * n + u + 1)
                if u == 0:
                    pe.wait_ge(v_done, n + 1)
                if h0 == 0:
                    if s or not first:
                        pe.wait_ge(ot_done, 4 * n + s)
                    if s == 0 and not first:
                        pe.wait_ge(gelu_done, NCH * (n - 1) + last_chunk(A) + 1)
                for kt in range(t + 1):
                    for i in range(HG[t]):
                        h = h0 + i
                        c0 = (i * (t + 1) + kt) * TT
                        v = v_cur[:, 2 * a + kt].rearrange("p b w -> p (b w)")[:, h * VW:(h + 1) * VW]
                        last = mm(A[VW * (h % 3):VW * (h % 3) + VW, 0:TT], v, pt_sb[:, u % 2, c0:c0 + TT],
                                  start=(kt == 0 and h < 3), stop=(kt == t and h >= 3), skip_group_check=True)
                last.then_inc(av_ready, 1)

            def project_out(n, s):
                pe.wait_ge(ot_done, 4 * n + s + 1)
                mm(M[:, 0:C], o_t[:], wp_sb[:], start=True, stop=True).then_inc(proj_ready, 1)

            def expert_out(n, parts):
                for s, c in parts:
                    dst = L2[s]
                    if c == 0:
                        if s == 3:
                            pe.wait_ge(comb, 16 * n + 8)
                        else:
                            pe.wait_ge(gelu_done, NCH * n + last_chunk(dst) + 1)
                        mm(dst[:, 0:E * C], ones2[:], b2hl[:], start=True, stop=False, skip_group_check=True)
                    if s == 0:
                        pe.wait_ge(gelu_done, NCH * n + c + 1)
                    e = c // CPE
                    last = mm(dst[:, e * C:(e + 1) * C], hid[:, c, s * TT:(s + 1) * TT], w2_sb[:, c],
                              start=False, stop=(c == NCH - 1), skip_group_check=True)
                    if c == NCH - 1:
                        last.then_inc(y_ready, 1)

            def expert_hidden(n, chunks, first):
                for c in chunks:
                    if c >= 4:
                        pe.wait_ge(gelu_done, NCH * n + c - 3)
                    elif c == 1:
                        pe.wait_ge(ot_done, 4 * n + 4)
                    elif not first:
                        pe.wait_ge(comb, 16 * n - 16 + 4 * (c + 1))
                    cs = slice(c * 128, (c + 1) * 128)
                    dst = L1[c % 4][:]
                    mm(dst, w1hi[:, cs], x2hi[:], start=True, stop=False)
                    mm(dst, w1lo[:, cs], x2hi[:], start=False, stop=False)
                    if c == 0:
                        pe.wait_ge(x2lo_done, n + 1)
                    mm(dst, w1hi[:, cs], x2lo[:], start=False, stop=True).then_inc(hid_ready, 1)

            def body(n, first=False, last=False):
                tail = [divmod(i, NCH) for i in range(SPB * NCH - TAIL, SPB * NCH)]
                for j in range(NU):
                    if j:
                        if j + 2 < NU:
                            scores(n, j + 2)
                        if not first:
                            expert_out(n - 1, out_parts(j))
                        values(n, j - 1, first)
                    else:
                        start = [] if first else out_parts(0)
                        expert_out(n - 1, start[:NCH])
                        scores(n, 2)
                        expert_out(n - 1, start[NCH:])
                    probs_t(n, j, first)
                    if j == EARLY_T0 and not last:
                        pe.wait_ge(v_done, n + 1)
                        tokens_first(n + 1)
                    if j == EARLY_XT and not last:
                        pe.wait_ge(t1_done, 4 * n + 1)
                        channels_first(n + 1)
                    for s in range(SPB - 1):
                        if j == TILE_END[s] + 1:
                            if last:
                                if s:
                                    pe.wait_ge(t1_done, 4 * n + s)
                                else:
                                    pe.wait_ge(v_done, n + 1)
                            elif s == 0:
                                pe.wait_ge(t0_done, n + 2)
                            elif s == 1:
                                pe.wait_ge(x1lo_done, n + 2)
                            else:
                                pe.wait_ge(t1_done, 4 * n + s)
                            project_out(n, s)
                if not last:
                    pe.wait_ge(exp_done, NU * n + NU)
                    project_q(n + 1)
                values(n, NU - 1, first)
                if not last:
                    project_k(n + 1)
                pe.wait_ge(t1_done, 4 * n + 3)
                project_out(n, SPB - 1)
                if not first:
                    expert_out(n - 1, tail[0:TAIL_EARLY])
                pe.wait_ge(xh2_done, 4 * n + 4)
                pe.wait_ge(pt_done, NU * n + NU)
                for s in range(SPB):
                    ins = nc.tensor.transpose(T[0:C, s * TT:(s + 1) * TT], xh2[:, s], id_sb[:])
                ins.then_inc(x2t_ready, 1)
                if not first:
                    expert_out(n - 1, tail[TAIL_EARLY:])
                if first:
                    pe.wait_ge(w_dve, W_ALL)
                pe.wait_ge(x2hi_done, n + 1)
                expert_hidden(n, range(0, 3), first)
                pe.wait_ge(t1_done, 4 * n + 4)
                split3(M[:], whi[:, 2 * C:], wlo[:, 2 * C:], x2hi[:], x2lo[:]).then_inc(route_ready, 1)
                expert_hidden(n, range(3, 6), first)
                wait_alone(pe, route_copied, n + 1)
                for s in range(SPB):
                    ins = nc.tensor.transpose(M[:, s * E:(s + 1) * E], gt_sb[:, s * TT:(s + 1) * TT], id_sb[0:E, 0:E])
                ins.then_inc(route_t_ready, 1)
                expert_hidden(n, range(6, 9), first)
                if not last:
                    scores(n + 1, 0)
                expert_hidden(n, range(9, NCH), first)
                if not last:
                    pe.wait_ge(route_dve, GATE_STEPS * n + 1)
                    project_v(n + 1)
                    scores(n + 1, 1)

            pe.wait_ge(t_half, STEPS)
            tokens_first(0)
            pe.wait_ge(t0_done, 1)
            channels_first(0)
            pe.wait_ge(w_dve, W_QK)
            pe.wait_ge(x1lo_done, 1)
            project_k(0)
            project_q(0)
            project_v(0)
            scores(0, 0)
            scores(0, 1)
            body(0, first=True)
            with pe.Fori(1, NBLK - 1) as n:
                body(n)
            body(NBLK - 1, last=True)
            for s in range(SPB):
                expert_out(NBLK - 1, [(s, c) for c in range(NCH)])


def kernel(x, L0_conv_w_i2s, L0_conv_w_s2s, L0_conv_w_skip, L0_conv_b_skip, L1_attn_Wq, L1_attn_Wk, L1_attn_Wv,
           L1_attn_Wp, L1_attn_bp, L1_ffn_gate_w, L1_ffn_gate_b, L1_ffn_w1, L1_ffn_b1, L1_ffn_w2, L1_ffn_b2):
    import ml_dtypes
    import numpy as np
    import concourse.bacc as bacc
    from concourse.bass_utils import run_bass_kernel_spmd

    f = np.float32
    bf = ml_dtypes.bfloat16
    GROUP = 3
    a = {}
    xp = np.zeros((C, ROWS, B, PADW), f)
    xp[:, :, :, 1:] = np.asarray(x).transpose(1, 2, 0, 3)
    a["x"] = xp.reshape(C, -1)
    per = FEAT // GROUP
    w = np.asarray(L0_conv_w_i2s)[:, :, 0, 0:2].reshape(GROUP, 4, per, C, 2).transpose(3, 4, 1, 0, 2)
    w = w.reshape(C, 2, 4, FEAT)
    wi = np.zeros((C, 2, 2, GATE_M), f)
    ws_a = np.zeros((GATE_M, 2, GATE_M), f)
    ws_b = np.zeros((GATE_M, 2, GATE_M), f)
    s2s = np.asarray(L0_conv_w_s2s)[:, :, 0, :].reshape(4, FEAT, FEAT, 3).transpose(2, 3, 0, 1)
    group = np.arange(C) * GROUP // C
    seen = (np.repeat(np.arange(GROUP), per)[None, :] >= group[:, None]).astype(f)
    wi_mask = np.zeros((C, 2, GATE_M), f)
    for g in range(4):
        c, o = g // 2, 64 * (g % 2)
        wi[:, :, c, o:o + FEAT] = w[:, :, g]
        wi_mask[:, c, o:o + FEAT] = seen
        ws_a[0:FEAT, c, o:o + FEAT] = s2s[:, 0, g]
        ws_a[64:, c, o:o + FEAT] = s2s[:, 1, g]
        ws_b[0:FEAT, c, o:o + FEAT] = s2s[:, 2, g]
    a["w_input"] = np.concatenate([wi.reshape(C, 4, GATE_M), wi_mask], axis=1)
    wk_skip, skip_mask = np.zeros((GATE_M, C), f), np.zeros((GATE_M, C), f)
    wk_skip[0:FEAT] = np.asarray(L0_conv_w_skip)[:, :, 0, 0].T
    skip_mask[0:FEAT] = group[None, :] >= (np.arange(FEAT) * GROUP // FEAT)[:, None]
    a["w_state"] = np.concatenate([ws_a.reshape(GATE_M, -1), ws_b.reshape(GATE_M, -1), wk_skip, skip_mask], axis=1)
    a["b_skip"] = np.asarray(L0_conv_b_skip).reshape(C, 1)
    a["wq"], a["wk"], a["wv"] = (np.asarray(z).transpose(1, 0, 2).reshape(C, C)
                                 for z in (L1_attn_Wq, L1_attn_Wk, L1_attn_Wv))
    a["wp"] = np.asarray(L1_attn_Wp).reshape(2, 3, HS, C).transpose(1, 0, 2, 3).reshape(C, C)
    a["bp"] = np.broadcast_to(np.asarray(L1_attn_bp), (128, C))
    gw = np.zeros((C, 128), f)
    gw[:, 0:E] = np.asarray(L1_ffn_gate_w)
    a["gate_w"] = gw
    a["gate_b"] = np.broadcast_to(np.tile(np.asarray(L1_ffn_gate_b), SPB), (128, SPB * E))
    a["w1"] = np.asarray(L1_ffn_w1).transpose(1, 0, 2).reshape(C, E * HID)
    a["b1"] = np.asarray(L1_ffn_b1).reshape(NCH, 128).T
    a["w2"] = np.asarray(L1_ffn_w2).reshape(NCH, 128, C).transpose(1, 0, 2)
    a["b2"] = np.broadcast_to(np.asarray(L1_ffn_b2).reshape(1, E * C), (2, E * C))
    a["ident"] = np.eye(128, dtype=f)
    a["ident_bf"] = np.eye(128).astype(bf)
    t, k = np.arange(TT)[:, None], np.arange(TT)[None, :]
    masked = np.where(k <= t, 0.0, float(ml_dtypes.finfo(bf).min)).astype(bf)
    a["causal_bf"] = np.broadcast_to(masked[:, None, :], (128, HG[0], TT))
    e, j = np.arange(E)[:, None], np.arange(E)[None, :]
    a["lower"] = np.broadcast_to((j < e).astype(f).reshape(1, E * E), (128, E * E))

    nc = bacc.Bacc("TRN2", target_bir_lowering=False, num_devices=1)
    arrays, args = {}, {}
    for name, v in a.items():
        v = np.ascontiguousarray(v)
        arrays[f"in_{name}"] = v
        args[name] = nc.dram_tensor(f"in_{name}", v.shape, mybir.dt.from_np(v.dtype), kind="ExternalInput").ap()
    args["out"] = nc.dram_tensor("out_y", (NBLK, 128, SPB, C), F32, kind="ExternalOutput").ap()
    hybrid_kernel(nc, **args)
    r = run_bass_kernel_spmd(nc, [arrays], core_ids=[0])
    y = r.results[0]["out_y"].reshape(NBLK, ROWS // 2, W, 2, 2, C)
    return y.transpose(0, 3, 5, 4, 1, 2).reshape(B, C, ROWS, W)
```
